# Optimizing a Trainium2 kernel written in Bass

```python
import numpy as np
import jax
import jax.numpy as jnp

def _softmax(x, axis=-1):
    return jax.nn.softmax(x, axis=axis)

def _gelu(x):
    return jax.nn.gelu(x, approximate=True)

def _silu(x):
    return jax.nn.silu(x)

def _sigmoid(x):
    return jax.nn.sigmoid(x)

def _layernorm(x, axis=-1, eps=1e-05):
    m = jnp.mean(x, axis=axis, keepdims=True)
    v = jnp.var(x, axis=axis, keepdims=True)
    return (x - m) / jnp.sqrt(v + eps)

def _scatter_add(tgt, idx, src, axis=0):
    return tgt.at[idx].add(src)

def _segment_sum(src, seg, n):
    return jax.ops.segment_sum(src, seg, n)
kernel_name = 'mk_prb_d1_jaxref_r8_d7edf2'

def setup_inputs(seed: int=0):
    np.random.seed(seed)
    _w = jnp.asarray

    def _L0_attn_setup():
        import jax, jax.numpy as jnp
        import numpy as np
        B, S, E, H = (2, 256, 256, 16)
        D = E // H
        NEG = -1e+30

        def alibi_slopes(n_heads):
            return jnp.asarray(2.0 ** (-8.0 * np.arange(1, n_heads + 1) / n_heads), dtype=jnp.float32)
        key = jax.random.key(seed)
        ks = jax.random.split(key, 5)
        sc = 0.02
        return {'x': jax.random.normal(ks[0], (B, S, E), dtype=jnp.float32), 'Wq': jax.random.normal(ks[1], (E, E), dtype=jnp.float32) * sc, 'Wk': jax.random.normal(ks[2], (E, E), dtype=jnp.float32) * sc, 'Wv': jax.random.normal(ks[3], (E, E), dtype=jnp.float32) * sc, 'Wo': jax.random.normal(ks[4], (E, E), dtype=jnp.float32) * sc, 'bo': jnp.zeros((E,), dtype=jnp.float32)}
    _L0_attn_in = _L0_attn_setup()

    def _L0_ffn_setup():
        import jax, jax.numpy as jnp
        import numpy as np
        TOP_K = 2
        key = jax.random.key(seed)
        ks = jax.random.split(key, 4)
        G, S, F, E, H = (4, 256, 256, 8, 256)
        return {'x': jax.random.normal(ks[0], (G, S, F), dtype=jnp.float32), 'router_logits': jax.random.normal(ks[1], (F, E), dtype=jnp.float32) * 0.02, 'gating_einsum': jax.random.normal(ks[2], (E, 2, H, F), dtype=jnp.float32) * 0.02, 'linear': jax.random.normal(ks[3], (E, H, F), dtype=jnp.float32) * 0.02, 'per_expert_scale': jnp.ones((E,), dtype=jnp.float32), 'router_scale': jnp.ones((F,), dtype=jnp.float32)}
    _L0_ffn_in = _L0_ffn_setup()
    _d = {'L0_attn_x': _L0_attn_in['x'], 'L0_attn_Wq': _L0_attn_in['Wq'], 'L0_attn_Wk': _L0_attn_in['Wk'], 'L0_attn_Wv': _L0_attn_in['Wv'], 'L0_attn_Wo': _L0_attn_in['Wo'], 'L0_attn_bo': _L0_attn_in['bo'], 'L0_ffn_router_logits': _L0_ffn_in['router_logits'], 'L0_ffn_gating_einsum': _L0_ffn_in['gating_einsum'], 'L0_ffn_linear': _L0_ffn_in['linear'], 'L0_ffn_per_expert_scale': _L0_ffn_in['per_expert_scale'], 'L0_ffn_router_scale': _L0_ffn_in['router_scale']}
    _x0 = _d['L0_attn_x']
    _d['L0_attn_x'] = jax.random.normal(jax.random.fold_in(jax.random.key(seed), 1), (4, 1024, 256), dtype=_x0.dtype)
    del _x0
    return _d

def reference(L0_attn_x, L0_attn_Wq, L0_attn_Wk, L0_attn_Wv, L0_attn_Wo, L0_attn_bo, L0_ffn_router_logits, L0_ffn_gating_einsum, L0_ffn_linear, L0_ffn_per_expert_scale, L0_ffn_router_scale):

    def _L0_attn_ref(x, Wq, Wk, Wv, Wo, bo):
        import jax, jax.numpy as jnp
        import numpy as np
        B, S, E, H = (2, 256, 256, 16)
        D = E // H
        NEG = -1e+30

        def alibi_slopes(n_heads):
            return jnp.asarray(2.0 ** (-8.0 * np.arange(1, n_heads + 1) / n_heads), dtype=jnp.float32)
        b, s, e = x.shape
        q = (x @ Wq).reshape(b, s, H, D).transpose(0, 2, 1, 3)
        k = (x @ Wk).reshape(b, s, H, D).transpose(0, 2, 1, 3)
        v = (x @ Wv).reshape(b, s, H, D).transpose(0, 2, 1, 3)
        scores = jnp.einsum('bhqd,bhkd->bhqk', q, k)
        i = jnp.arange(s)[:, None]
        j = jnp.arange(s)[None, :]
        causal = j <= i
        scores = jnp.where(causal[None, None], scores, NEG)
        bias = alibi_slopes(H)[:, None, None] * (j - i).astype(jnp.float32)
        scores = scores + bias[None]
        scores = scores / jnp.sqrt(jnp.float32(D))
        w = jax.nn.softmax(scores, axis=-1)
        ctx = jnp.einsum('bhqk,bhkd->bqhd', w, v).reshape(b, s, e)
        return ctx @ Wo + bo

    def _L0_ffn_ref(x, router_logits, gating_einsum, linear, per_expert_scale, router_scale):
        import jax, jax.numpy as jnp
        import numpy as np
        TOP_K = 2
        G, S, F = x.shape
        E = router_logits.shape[-1]
        H = linear.shape[1]
        k = TOP_K
        dtype = x.dtype
        var = jnp.mean(jnp.square(x.astype(jnp.float32)), axis=-1, keepdims=True)
        router_input = x * jax.lax.rsqrt(var + 1e-06).astype(dtype)
        root_size = jax.lax.rsqrt(jnp.array(F, dtype=dtype))
        router_input = router_input * root_size * router_scale.astype(dtype)
        logits = jnp.einsum('gsd,de->gse', router_input, router_logits.astype(dtype))
        logits32 = logits.astype(jnp.float32)
        probs = jax.nn.softmax(logits32, axis=-1)
        _, choices = jax.lax.approx_max_k(logits32, k=k)
        indicator = jax.nn.one_hot(choices, E, dtype=probs.dtype).sum(axis=-2)
        renorm = jnp.sum(indicator * probs, axis=-1, keepdims=True)
        renorm = jnp.where(renorm > 0.0, renorm, 1.0)
        weights = probs / renorm
        x_flat = x.reshape((-1, F))
        batch_size = G * S
        choices_flat = choices.ravel()
        xs_order = choices_flat.argsort()
        xs_reverse_argsort = xs_order.argsort()
        xs_indices = jnp.repeat(jnp.arange(batch_size), k)[xs_order]
        sorted_xs = x_flat[xs_indices, :]
        choices_oh = jax.nn.one_hot(choices, num_classes=E, dtype=jnp.int32)
        tokens_per_expert = jnp.sum(choices_oh, axis=(0, 1, 2))
        combine_weights = (choices_oh.astype(jnp.float32) * jnp.expand_dims(weights, axis=2)).sum(axis=-1).astype(weights.dtype)
        w_gate = jnp.transpose(gating_einsum, (0, 3, 1, 2)).reshape(E, F, 2 * H)
        gate_out = jax.lax.ragged_dot(sorted_xs, w_gate.astype(dtype), group_sizes=tokens_per_expert)
        gate_out = gate_out.reshape(gate_out.shape[0], 2, H)
        activation = jax.nn.gelu(gate_out[:, 0, :]) * gate_out[:, 1, :]
        expert_outputs = jax.lax.ragged_dot(activation, linear.astype(dtype), group_sizes=tokens_per_expert)
        expert_indices = jnp.repeat(jnp.arange(E), tokens_per_expert, total_repeat_length=expert_outputs.shape[0])
        expert_outputs = expert_outputs * per_expert_scale.astype(expert_outputs.dtype)[expert_indices, None]
        out = expert_outputs[xs_reverse_argsort].reshape((G, S, k, -1))
        out = jnp.einsum('blkd,blk->bld', out, combine_weights, preferred_element_type=out.dtype)
        return out
    x = L0_attn_x
    xn = _layernorm(x, axis=-1)
    x = x + _L0_attn_ref(xn, L0_attn_Wq, L0_attn_Wk, L0_attn_Wv, L0_attn_Wo, L0_attn_bo) + _L0_ffn_ref(xn, L0_ffn_router_logits, L0_ffn_gating_einsum, L0_ffn_linear, L0_ffn_per_expert_scale, L0_ffn_router_scale)
    return x

_drawn_inputs = setup_inputs


def setup_inputs(seed=0):
    import zlib

    import numpy as np

    out = dict(_drawn_inputs(seed))
    spreads = {'L0_attn_bo': (0.0, 0.1),
     'L0_ffn_per_expert_scale': (1.0, 0.6),
     'L0_ffn_router_scale': (1.0, 0.6)}
    factors = {'L0_attn_Wq': 8.0,
     'L0_attn_Wk': 8.0,
     'L0_attn_Wv': 3.573,
     'L0_attn_Wo': 3.581,
     'L0_ffn_router_logits': 5.078,
     'L0_ffn_gating_einsum': 4.379,
     'L0_ffn_linear': 4.382}
    for name, (base, spread) in spreads.items():
        noise = np.random.default_rng([zlib.crc32(name.encode()), seed]).standard_normal(out[name].shape)
        drawn = base * np.exp(spread * noise) if base else spread * noise
        out[name] = jnp.asarray(drawn.astype(out[name].dtype))
    for name, factor in factors.items():
        out[name] = (out[name] * factor).astype(out[name].dtype)
    return out
```

```python
from contextlib import ExitStack

import concourse.bass as bass
from concourse import mybir
import numpy as np

P = 128
F32 = mybir.dt.float32
BF16 = mybir.dt.bfloat16
I32 = mybir.dt.int32
U32 = mybir.dt.uint32
U16 = mybir.dt.uint16
ALU = mybir.AluOpType
ACT = mybir.ActivationFunctionType
AX_X = mybir.AxisListType.X
ds = bass.ds

B, S, D = 4, 1024, 256
NH, HD = 16, 16
TOK = B * S
NT = TOK // P
DH = D // P
NQ = NH // 4
NE, HID = 8, 256
CH = 512
NC = TOK // CH
NST = 2 * TOK // P + NE
LN_EPS, RMS_EPS = 1e-5, 1e-6
NEG = -1e30
KT = S // P

Q_PART = [0, 1, 2, 0, 1, 0]
K_PART = [0, 0, 0, 1, 1, 2]
R_ALIBI = 6 * HD
R_MAX = R_ALIBI + 6
ROWS = R_MAX + 3
VW = HD + 1
SCALE = float(HD) ** -0.5

UNITS = [
    [(0, 0, 0, 512)],
    [(0, 0, 512, 512)],
    [(0, 1, 128, 384), (384, 3, 384, 128)],
    [(0, 1, 512, 512)],
    [(0, 2, 256, 256), (256, 6, 768, 256)],
    [(0, 2, 512, 512)],
    [(0, 3, 512, 512)],
    [(0, 4, 512, 512)],
    [(0, 5, 640, 384), (384, 7, 896, 128)],
]
NU = len(UNITS)
DIAG = [[c for c, kt, q0, _ in u if q0 == kt * P] for u in UNITS]
MASKED = [sum(map(len, DIAG[:u])) for u in range(NU + 1)]
PRING = 3

ITEMS = [(h, qt) for h in range(4) for qt in (7, 0, 6, 1, 5, 2, 4, 3)]
NI = len(ITEMS) + 1
LEAD = 12
SLOTS = 4 * NU
FIRST_PART = 24


def slot_items():
    ahead1 = [(1, k) for k in range(LEAD, NI)]
    ahead2 = [(2, k) for k in range(LEAD)]
    out, done = [], 0
    for s in range(SLOTS):
        if s < FIRST_PART:
            upto = (s + 1) * len(ahead1) // FIRST_PART
            out.append(ahead1[done:upto])
            done = upto
        else:
            n = s - FIRST_PART
            out.append(ahead2[n:n + 1])
    return out


SLOT_ITEMS = slot_items()
assert sum(map(len, SLOT_ITEMS)) == NI


def project(nc, ins, scratch, keep):
    with ExitStack() as ctx:
        sb = lambda name, shape, dt=F32: ctx.enter_context(nc.sbuf_tensor(name, shape, dt))
        ps = lambda name, shape: ctx.enter_context(nc.psum_tensor(name, shape, F32))
        sem = lambda name: ctx.enter_context(nc.semaphore(name))
        w_qk = sb("w_qk", [P, DH, NQ, P])
        w_vr = sb("w_vr", [P, DH, D + NE])
        rscale = sb("rscale", [P, DH])
        ident, mhalf = keep["ident"], keep["mhalf"]
        x_in = sb("x_in", [P, 2, 4, D])
        xn = sb("xn", [P, 2, 4, D])
        stats = sb("stats", [P, 2, 4, 6])
        mv = sb("mv", [P, 2, 4, 2])
        veps = sb("veps", [P, 2, 4])
        rstd = sb("rstd", [P, 2, 4])
        rsq = sb("rsq", [P, 2, 4])
        xT = sb("xT", [P, 2, DH, CH])
        rest = sb("rest", [P, 2, CH])
        parts = sb("parts", [P, NQ, 3, CH], BF16)
        vt = sb("vt", [P, 2, 4, NQ, 4, VW])
        zeros = sb("zeros", [P, 2048])
        tpsum = ps("tpsum", [P, DH, CH])
        qkpsum = ps("qkpsum", [P, 2, CH])
        vpsum = ps("vpsum", [P, 2, CH])

        weights_in = sem("weights_in")
        zeros_set = sem("zeros_set")
        const_set = sem("const_set")
        rweight_set = sem("rweight_set")
        ones_set = sem("ones_set")
        passed = sem("passed1")
        x_loaded = [sem(f"x_loaded{i}") for i in range(2)]
        x_stored = [sem(f"x_stored{i}") for i in range(2)]
        parts_stored = [sem(f"parts_stored{i}") for i in range(NQ)]
        v_stored = [sem(f"v_stored{i}") for i in range(2)]
        zeros_stored = sem("zeros_stored")
        dve_step = sem("dve_step")
        pool_step = sem("pool_step")
        mv_ready = sem("mv_ready")
        rstd_ready = sem("rstd_ready")
        xn_ready = sem("xn_ready")
        tp_ready = sem("tp_ready")
        xT0_ready = sem("xT0_ready")
        xT1_ready = sem("xT1_ready")
        qk_ready = sem("qk_ready")
        p1_ready = sem("p1_ready")
        rest_ready = sem("rest_ready")
        p2_ready = sem("p2_ready")
        p3_ready = sem("p3_ready")
        v_ready = sem("v_ready")
        v_taken = sem("v_taken")
        block = ctx.enter_context(nc.Block())

        RING = 2

        def chunks(eng, body):
            with eng.Fori(0, NC // 2 - 1) as i:
                body(2 * i, 0, True, i)
                body(2 * i + 1, 1, True, i)
            body(NC - 2, 0, True, NC // 2 - 1)
            body(NC - 1, 1, False, NC // 2 - 1)

        x_rows = ins["x"].rearrange("(c t p) d -> c p t d", c=NC, p=P)
        xn_rows = scratch["xn"].rearrange("(c t p) d -> c p t d", c=NC, p=P)
        n_zero = NST * P * D // (P * 2048)

        @block.sync
        def _(sp):
            for i in range(2):
                sp.sem_inc(x_stored[i], 16)
                sp.sem_inc(v_stored[i], 16 * NQ)
                sp.dma_start(x_in[:, i], x_rows[i]).then_inc(x_loaded[i], 16)
            for q in range(NQ):
                sp.sem_inc(parts_stored[q], 16)
            sp.dma_start(w_vr[:, :, 0:D], ins["w_v"]).then_inc(weights_in, 16)
            sp.dma_start(w_vr[:, :, D:D + NE], ins["w_r"]).then_inc(weights_in, 16)
            sp.dma_start(rscale[:, :], ins["router_scale"]).then_inc(weights_in, 16)
            sp.dma_start(w_qk[:, :, :, :], ins["w_qk"]).then_inc(weights_in, 16)

            def stores(c, par, load):
                sp.wait_ge(xn_ready, c + 1)
                sp.dma_start(xn_rows[ds(c, 1)].rearrange("a p t d -> (a p) t d"), xn[:, par]).then_inc(x_stored[par], 16)
                if load:
                    sp.dma_start(x_in[:, par], x_rows[ds(c + 2, 1)].rearrange("a p t d -> (a p) t d")).then_inc(x_loaded[par], 16)
                for q in range(NQ):
                    sp.wait_ge(p3_ready, 4 * c + q + 1 + RING)
                    sp.dma_start(scratch["qk"][q].rearrange("a p t -> p a t")[:, :, ds(CH * c, CH)],
                                 parts[:, q]).then_inc(parts_stored[q], 16)
                sp.wait_ge(v_taken, 4 * c + 4 + RING)
                for q in range(NQ):
                    sp.dma_start(scratch["v"][q].rearrange("(t p) w -> p t w", p=P)[:, ds(4 * c, 4), :],
                                 vt[:, par, :, q].rearrange("p t h w -> p t (h w)")).then_inc(v_stored[par], 16)

            with sp.Fori(0, NC // 2 - 1) as i:
                stores(2 * i, 0, True)
                stores(2 * i + 1, 1, True)
            sp.wait_ge(zeros_set, 1)
            flat = scratch["xs"].rearrange("(n p r) d -> n p (r d)", n=n_zero, p=P)
            for j in range(n_zero):
                sp.dma_start(flat[j], zeros[:, :]).then_inc(zeros_stored, 16)
            stores(NC - 2, 0, False)
            stores(NC - 1, 1, False)
            for i in range(2):
                sp.wait_ge(x_stored[i], 16 + 16 * (NC // 2))
                sp.wait_ge(v_stored[i], 16 * NQ * (1 + NC // 2))
            for q in range(NQ):
                sp.wait_ge(parts_stored[q], 16 + 16 * NC)
            sp.wait_ge(zeros_stored, 16 * n_zero)

        @block.gpsimd
        def _(pool):
            pool.sem_inc(p3_ready, RING)
            pool.memset(ident[:, :], 0.0).then_inc(pool_step, 1)
            pool.memset(mhalf[:, :], -0.5).then_inc(const_set, 1)
            pool.wait_ge(pool_step, 1)
            pool.affine_select(out=ident[:, :], in_=ident[:, :], compare_op=ALU.not_equal, fill=1.0,
                               base=0, pattern=[[-1, P]], channel_multiplier=1).then_inc(const_set, 1)
            pool.memset(vt[:, :, :, :, :, :].rearrange("p b t q h w -> p (b t q h) w")[:, :, HD:VW], 1.0).then_inc(ones_set, 1)
            pool.wait_ge(const_set, 2)
            STEPS = 3

            def rstds(c, par):
                k = 1 + STEPS * c
                pool.wait_ge(mv_ready, c + 1)
                pool.sem_inc(passed, 1)
                pool.tensor_scalar(veps[:, par], mv[:, par, :, 1], LN_EPS, None, ALU.add).then_inc(pool_step, 1)
                pool.wait_ge(pool_step, k + 1)
                pool.tensor_tensor(rstd[:, par], veps[:, par], mhalf[:, 0:4], ALU.pow).then_inc(rstd_ready, 1)
                pool.wait_ge(rstd_ready, c + 1)
                pool.tensor_tensor(rsq[:, par], rstd[:, par], rstd[:, par], ALU.mult).then_inc(pool_step, 1)
                pool.wait_ge(pool_step, k + 2)
                pool.tensor_tensor(keep["msq"][:, ds(4 * c, 4)], rsq[:, par], mv[:, par, :, 1], ALU.mult).then_inc(pool_step, 1)

            rstds(0, 0)
            pool.memset(zeros[:, :], 0.0).then_inc(zeros_set, 1)

            def body(c, par, nxt, i):
                if nxt:
                    rstds(c + 1, 1 - par)
                for q in range(NQ):
                    pool.wait_ge(p2_ready, 4 * c + q + 1)
                    pool.tensor_tensor(parts[:, q, 2], rest[:, q % 2], parts[:, q, 1], ALU.subtract).then_inc(p3_ready, 1)

            chunks(pool, body)

        @block.vector
        def _(dve):
            dve.sem_inc(rest_ready, RING)
            dve.wait_ge(weights_in, 64)
            for dh in range(DH):
                last = dve.tensor_scalar(w_vr[:, dh, D:D + NE], w_vr[:, dh, D:D + NE], rscale[:, dh:dh + 1], None, ALU.mult)
            last.then_inc(rweight_set, 1)

            def normalise(c, par, i):
                dve.wait_ge(x_loaded[par], 16 * (i + 1))
                for t in range(4):
                    last = dve.bn_stats(stats[:, par, t], x_in[:, par, t])
                last.then_inc(dve_step, 1)
                dve.wait_ge(dve_step, c + 1)
                dve.sem_inc(passed, 1)
                for t in range(4):
                    last = dve.bn_aggr(mv[:, par, t], stats[:, par, t])
                last.then_inc(mv_ready, 1)
                dve.wait_ge(mv_ready, c + 1)
                dve.wait_ge(rstd_ready, c + 1)
                dve.wait_ge(x_stored[par], 16 * (i + 1))
                for t in range(4):
                    last = dve.tensor_scalar(xn[:, par, t], x_in[:, par, t], mv[:, par, t, 0:1],
                                             rstd[:, par, t:t + 1], ALU.subtract, ALU.mult)
                last.then_inc(xn_ready, 1)

            def evacuate(c, par):
                dve.wait_ge(tp_ready, 2 * c + 2)
                dve.tensor_copy(xT[:, par, 1], tpsum[:, 1]).then_inc(xT1_ready, 1)

            normalise(0, 0, 0)
            evacuate(0, 0)

            def body(c, par, nxt, i):
                if nxt:
                    normalise(c + 1, 1 - par, i + par)
                for q in range(NQ):
                    n = 4 * c + q
                    dve.wait_ge(p1_ready, n + 1)
                    dve.wait_ge(p3_ready, n + 1)
                    dve.tensor_tensor(rest[:, q % 2], qkpsum[:, q % 2], parts[:, q, 0], ALU.subtract).then_inc(rest_ready, 1)
                    dve.wait_ge(rest_ready, n + 1 + RING)
                    dve.tensor_copy(parts[:, q, 1], rest[:, q % 2]).then_inc(p2_ready, 1)
                if nxt:
                    evacuate(c + 1, 1 - par)

            chunks(dve, body)

        @block.scalar
        def _(act):
            act.sem_inc(v_taken, RING)

            def evacuate(c, par):
                act.wait_ge(tp_ready, 2 * c + 1)
                act.activation(xT[:, par, 0], tpsum[:, 0], ACT.Copy).then_inc(xT0_ready, 1)

            evacuate(0, 0)
            act.wait_ge(ones_set, 1)

            def body(c, par, nxt, i):
                for q in range(NQ):
                    n = 4 * c + q
                    act.wait_ge(qk_ready, n + 1)
                    act.wait_ge(parts_stored[q], 16 * (c + 1))
                    act.activation(parts[:, q, 0], qkpsum[:, q % 2], ACT.Copy).then_inc(p1_ready, 1)
                if nxt:
                    evacuate(c + 1, 1 - par)
                act.wait_ge(v_stored[par], 16 * NQ * (i + 1))
                for t in range(4):
                    act.wait_ge(v_ready, 4 * c + t + 1)
                    act.activation(vt[:, par, t].rearrange("p q h w -> p (q h) w")[:, :, 0:HD],
                                   vpsum[:, t % 2, 0:D].rearrange("p (g w) -> p g w", w=HD), ACT.Copy)
                    act.activation(keep["logits"][:, ds(4 * c + t, 1), :].rearrange("p a e -> p (a e)"),
                                   vpsum[:, t % 2, D:D + NE], ACT.Copy).then_inc(v_taken, 1)

            chunks(act, body)

        @block.tensor
        def _(pe):
            pe.wait_ge(const_set, 2)

            def transposes(c, par):
                pe.wait_ge(xn_ready, c + 1)
                for dh in range(DH):
                    for t in range(4):
                        last = pe.transpose(tpsum[:, dh, t * P:(t + 1) * P], xn[:, par, t, dh * P:(dh + 1) * P], ident[:, :])
                    last.then_inc(tp_ready, 1)

            transposes(0, 0)
            pe.wait_ge(weights_in, 64)
            pe.wait_ge(rweight_set, 1)

            def body(c, par, nxt, i):
                pe.wait_ge(xT0_ready, c + 1)
                pe.wait_ge(xT1_ready, c + 1)
                for q in range(NQ):
                    pe.wait_ge(rest_ready, 4 * c + q + 1)
                    for dh in range(DH):
                        last = pe.matmul(qkpsum[:, q % 2], w_qk[:, dh, q], xT[:, par, dh], start=dh == 0, stop=dh == DH - 1)
                    last.then_inc(qk_ready, 1)
                if nxt:
                    transposes(c + 1, 1 - par)
                for t in range(4):
                    pe.wait_ge(v_taken, 4 * c + t + 1)
                    for dh in range(DH):
                        last = pe.matmul(vpsum[:, t % 2, 0:D + NE], xT[:, par, dh, t * P:(t + 1) * P], w_vr[:, dh],
                                         start=dh == 0, stop=dh == DH - 1)
                    last.then_inc(v_ready, 1)

            chunks(pe, body)


def route(nc, ins, scratch, keep):
    with ExitStack() as ctx:
        sb = lambda name, shape, dt=F32: ctx.enter_context(nc.sbuf_tensor(name, shape, dt))
        sem = lambda name: ctx.enter_context(nc.semaphore(name))
        counts = ctx.enter_context(nc.psum_tensor("counts", [P, 2, CH], F32))
        E3 = [P, NT, NE]
        msqe, rms = sb("msqe", [P, NT]), sb("rms", [P, NT])
        logit = sb("logit", E3)
        top = [sb(f"top{k}", [P, NT]) for k in range(2)]
        hit, key = sb("hit", E3), sb("key", E3)
        first = sb("first", [P, NT])
        chosen = [sb(f"chosen{k}", E3) for k in range(2)]
        masked = sb("masked", E3)
        expd, prob = sb("expd", E3), sb("prob", E3)
        esum = sb("esum", [P, NT])
        picked = sb("picked", E3)
        pk = [sb(f"pk{k}", [P, NT]) for k in range(2)]
        renorm, guard = sb("renorm", [P, NT]), sb("guard", [P, NT])
        escale = sb("escale", [P, NE])
        sk = sb("sk", [P, NT])
        rank_of, reset = sb("rank_of", [P, NE]), sb("reset", [P, NE, NT])
        both = sb("both", E3, BF16)
        tri, ones = sb("tri", [P, P], BF16), sb("ones", [P, P], BF16)
        cnt, run = sb("cnt", [P, NE, NT]), sb("run", [P, NE, NT])
        pos = sb("pos", [P, NE, NT])
        total, total_i = sb("total", [P, NE]), sb("total_i", [P, NE], I32)
        tiles_i, tiles = sb("tiles_i", [P, NE], I32), sb("tiles", [P, NE])
        ends, base = sb("ends", [P, NE]), sb("base", [P, NE])
        slot_f = sb("slot_f", [P, NT])
        tile_no, past = sb("tile_no", [1, NST, NE]), sb("past", [1, NST, NE])
        tile_f = sb("tile_f", [1, NST])
        scale_in = sem("scale_in")
        pool_set = sem("pool_set")
        rms_ready = sem("rms_ready")
        pool_step = sem("pool_step_r")
        dve_step = sem("dve_step_r")
        shifted = sem("shifted")
        exp_ready = sem("exp_ready")
        both_ready = sem("both_ready")
        counted = sem("counted")
        routed = sem("routed")
        block = ctx.enter_context(nc.Block())
        per_expert = lambda a: a.rearrange("p (t a) -> p t a", a=1).to_broadcast(E3)

        @block.sync
        def _(sp):
            sp.dma_start(escale[:, :], ins["expert_scale"].partition_broadcast(P)).then_inc(scale_in, 16)
            sp.wait_ge(scale_in, 16)

        @block.gpsimd
        def _(pool):
            pool.tensor_scalar(msqe[:, :], keep["msq"][:, :], RMS_EPS, None, ALU.add).then_inc(pool_step, 1)
            pool.wait_ge(pool_step, 1)
            pool.tensor_tensor(rms[:, :], msqe[:, :], keep["mhalf"][:, 0:NT], ALU.pow).then_inc(rms_ready, 1)
            pool.iota(rank_of[:, :], pattern=[[-1, NE]], base=NE, channel_multiplier=0, allow_small_or_imprecise_dtypes=True).then_inc(pool_set, 1)
            pool.iota(tile_no[:, :, :], pattern=[[1, NST], [0, NE]], base=0, channel_multiplier=0, allow_small_or_imprecise_dtypes=True).then_inc(pool_set, 1)
            pool.memset(reset[:, :, :], 1.0).then_inc(pool_step, 1)
            pool.memset(ones[:, :], 1.0).then_inc(pool_set, 1)
            pool.wait_ge(pool_step, 2)
            pool.memset(reset[:, :, 0:1], 0.0).then_inc(pool_set, 1)
            pool.wait_ge(pool_set, 4)
            pool.affine_select(out=tri[:, :], in_=ones[:, :], compare_op=ALU.is_gt, fill=0.0,
                               base=0, pattern=[[1, P]], channel_multiplier=-1).then_inc(pool_set, 1)
            mask = keep["mask"]
            pool.memset(mask[:, :], 0.0).then_inc(pool_step, 1)
            pool.wait_ge(pool_step, 3)
            pool.affine_select(out=mask[:, :], in_=mask[:, :], compare_op=ALU.is_ge, fill=NEG,
                               base=S - P, pattern=[[-1, S]], channel_multiplier=1).then_inc(pool_set, 1)

        @block.tensor
        def _(pe):
            pe.wait_ge(pool_set, 5)
            pe.wait_ge(both_ready, 1)
            rhs = both[:, :, :].rearrange("p t e -> p (t e)")
            pe.matmul(counts[:, 0, 0:NT * NE], tri[:, :], rhs, start=True, stop=True)
            pe.matmul(counts[:, 1, 0:NT * NE], ones[:, :], rhs, start=True, stop=True).then_inc(counted, 1)

        @block.scalar
        def _(act):
            act.wait_ge(shifted, 1)
            act.activation(expd[:, :, :], expd[:, :, :], ACT.Exp).then_inc(exp_ready, 1)

        @block.vector
        def _(dve):
            steps = [0]

            def then(ins_):
                ins_.then_inc(dve_step, 1)
                steps[0] += 1
                dve.wait_ge(dve_step, steps[0])

            dve.wait_ge(rms_ready, 1)
            dve.wait_ge(pool_set, 6)
            dve.wait_ge(scale_in, 16)
            then(dve.tensor_scalar(rms[:, :], rms[:, :], float(D) ** -0.5, None, ALU.mult))
            then(dve.tensor_tensor(logit[:, :, :], keep["logits"][:, :, :], per_expert(rms[:, :]), ALU.mult))
            src = logit
            rank3 = rank_of[:, :].rearrange("p (a e) -> p a e", a=1).to_broadcast(E3)
            for k in range(2):
                then(dve.tensor_reduce(top[k][:, :], src[:, :, :], AX_X, ALU.max))
                then(dve.tensor_tensor(hit[:, :, :], src[:, :, :], per_expert(top[k][:, :]), ALU.is_equal))
                then(dve.tensor_tensor(key[:, :, :], hit[:, :, :], rank3, ALU.mult))
                then(dve.tensor_reduce(first[:, :], key[:, :, :], AX_X, ALU.max))
                then(dve.tensor_tensor(chosen[k][:, :, :], rank3, per_expert(first[:, :]), ALU.is_equal))
                if k == 0:
                    then(dve.scalar_tensor_tensor(masked[:, :, :].rearrange("p t e -> p (t e)"),
                                                  chosen[0][:, :, :].rearrange("p t e -> p (t e)"), NEG,
                                                  logit[:, :, :].rearrange("p t e -> p (t e)"), ALU.mult, ALU.add))
                    src = masked
            dve.tensor_tensor(expd[:, :, :], logit[:, :, :], per_expert(top[0][:, :]), ALU.subtract).then_inc(shifted, 1)
            dve.tensor_tensor(both[:, :, :], chosen[0][:, :, :], chosen[1][:, :, :], ALU.add).then_inc(both_ready, 1)
            dve.wait_ge(exp_ready, 1)
            then(dve.tensor_reduce(esum[:, :], expd[:, :, :], AX_X, ALU.add))
            then(dve.reciprocal(esum[:, :], esum[:, :]))
            then(dve.tensor_tensor(prob[:, :, :], expd[:, :, :], per_expert(esum[:, :]), ALU.mult))
            for k in range(2):
                then(dve.tensor_tensor(picked[:, :, :], prob[:, :, :], chosen[k][:, :, :], ALU.mult))
                then(dve.tensor_reduce(pk[k][:, :], picked[:, :, :], AX_X, ALU.add))
            then(dve.tensor_tensor(renorm[:, :], pk[0][:, :], pk[1][:, :], ALU.add))
            then(dve.tensor_scalar(guard[:, :], renorm[:, :], 0.0, None, ALU.is_le))
            then(dve.tensor_tensor(renorm[:, :], renorm[:, :], guard[:, :], ALU.add))
            then(dve.reciprocal(renorm[:, :], renorm[:, :]))
            scale3 = escale[:, :].rearrange("p (a e) -> p a e", a=1).to_broadcast(E3)
            for k in range(2):
                then(dve.tensor_tensor(picked[:, :, :], scale3, chosen[k][:, :, :], ALU.mult))
                then(dve.tensor_reduce(sk[:, :], picked[:, :, :], AX_X, ALU.add))
                then(dve.tensor_tensor(sk[:, :], sk[:, :], renorm[:, :], ALU.mult))
                then(dve.tensor_tensor(keep["weight"][:, k], sk[:, :], pk[k][:, :], ALU.mult))
            dve.wait_ge(counted, 1)
            view = lambda j: counts[:, j, 0:NT * NE].rearrange("p (t e) -> p e t", e=NE)
            then(dve.tensor_copy(cnt[:, :, :], view(1)))
            flat = lambda a: a[:, :, :].rearrange("p e t -> p (e t)")
            then(dve.tensor_tensor_scan(flat(run), flat(reset), flat(cnt), 0.0, ALU.mult, ALU.add))
            then(dve.tensor_scalar(total[:, :], run[:, :, NT - 1], float(P - 1), None, ALU.add))
            then(dve.tensor_copy(total_i[:, :], total[:, :]))
            then(dve.tensor_scalar(tiles_i[:, :], total_i[:, :], P.bit_length() - 1, None, ALU.arith_shift_right))
            then(dve.tensor_copy(tiles[:, :], tiles_i[:, :]))
            then(dve.tensor_tensor_scan(ends[:, :], reset[:, 0, 1:NE + 1], tiles[:, :], 0.0, ALU.mult, ALU.add))
            then(dve.tensor_tensor(base[:, :], ends[:, :], tiles[:, :], ALU.subtract))
            then(dve.tensor_scalar(base[:, :], base[:, :], float(P), None, ALU.mult))
            then(dve.tensor_tensor(pos[:, :, :], run[:, :, :], cnt[:, :, :], ALU.subtract))
            then(dve.tensor_tensor(pos[:, :, :], pos[:, :, :], view(0), ALU.add))
            then(dve.tensor_tensor(pos[:, :, :], pos[:, :, :], base[:, :].rearrange("p (e a) -> p e a", a=1).to_broadcast([P, NE, NT]), ALU.add))
            for k in range(2):
                then(dve.tensor_tensor(picked[:, :, :], pos[:, :, :].rearrange("p e t -> p t e"), chosen[k][:, :, :], ALU.mult))
                then(dve.tensor_reduce(slot_f[:, :], picked[:, :, :], AX_X, ALU.add))
                then(dve.tensor_copy(keep["slot"][:, k], slot_f[:, :]))
            then(dve.tensor_tensor(past[:, :, :], tile_no[:, :, :], ends[0:1, :].rearrange("p (a e) -> p a e", a=1).to_broadcast([1, NST, NE]), ALU.is_ge))
            then(dve.tensor_reduce(tile_f[:, :], past[:, :, :], AX_X, ALU.add))
            dve.tensor_scalar(keep["tile_expert"][:, :], tile_f[:, :], float(NE - 1), None, ALU.min).then_inc(routed, 1)
            dve.wait_ge(routed, 1)


def attend(nc, ins, scratch, keep):
    with ExitStack() as ctx:
        sb = lambda name, shape, dt=F32: ctx.enter_context(nc.sbuf_tensor(name, shape, dt))
        sem = lambda name: ctx.enter_context(nc.semaphore(name))
        qs = [sb(f"qs{i}", [ROWS, 4, S], BF16) for i in range(NQ)]
        ks = [sb(f"ks{i}", [ROWS, 4, S], BF16) for i in range(NQ)]
        vs = [sb(f"vs{i}", [P, KT, 4, VW]) for i in range(NQ)]
        probs = sb("probs", [P, PRING, 4, CH])
        junk = sb("junk", [P, 2, S], BF16)
        maxima = sb("maxima", [P, 2, 4, KT])
        mrest = sb("mrest", [4 * KT, P])
        mparts = sb("mparts", [4 * KT, 2, 3, P], BF16)
        xrows = sb("xrows", [P, 2, 2, D])
        slots = sb("slots", [P, 2, 2, 2], I32)
        mpsum = ctx.enter_context(nc.psum_tensor("mpsum", [P, 2, S], F32))
        spsum = ctx.enter_context(nc.psum_tensor("spsum", [P, 2, CH], F32))
        cpsum = ctx.enter_context(nc.psum_tensor("cpsum", [P, 2, CH], F32))

        stack_in = [sem(f"stack_in{i}") for i in range(NQ)]
        const_in = sem("const_in")
        v_in = [sem(f"v_in{i}") for i in range(NQ)]
        mrow_in = [sem(f"mrow_in{i}") for i in range(NQ)]
        cleared = sem("cleared")
        passed = sem("passed3")
        m_ready = sem("m_ready")
        m_taken = sem("m_taken")
        max_step = sem("max_step")
        max_split = sem("max_split")
        s_ready = sem("s_ready")
        exp_done = sem("exp_done")
        masked = sem("masked")
        pv_done = sem("pv_done")
        ctx_taken = sem("ctx_taken")
        rows_in = [sem(f"rows_in{i}") for i in range(2)]
        rows_out = [sem(f"rows_out{i}") for i in range(2)]
        block = ctx.enter_context(nc.Block())
        RING = 2

        def wait_apart(eng, sem, value):
            eng.wait_ge(sem, value)
            eng.sem_inc(passed, 1)

        STACK_DMAS = 2 * len(Q_PART)

        def steps(eng, body):
            with eng.Fori(0, B - 1) as b:
                for hq in range(NQ):
                    body(NQ * b + hq, b, hq, lambda j: True)
            for hq in range(NQ):
                body(NQ * (B - 1) + hq, B - 1, hq, lambda j, hq=hq: hq + j < NQ)

        def quad(b, hq, j):
            return b + (hq + j) // NQ, (hq + j) % NQ

        @block.sync
        def _(sp):
            for q in range(NQ):
                sp.dma_start(qs[q][R_ALIBI:R_MAX, :, :], ins["c_q"][q]).then_inc(const_in, 16)
                sp.dma_start(ks[q][R_ALIBI:ROWS, :, :], ins["c_k"]).then_inc(const_in, 16)

            def load(b, hq):
                parts_of = scratch["qk"][hq]
                for r in range(len(Q_PART)):
                    for side, dst, part in ((0, qs[hq], Q_PART[r]), (1, ks[hq], K_PART[r])):
                        src = parts_of[part, 4 * HD * side:4 * HD * (side + 1), ds(S * b, S)]
                        sp.dma_start(dst[HD * r:HD * (r + 1), :, :], src.rearrange("(h d) t -> d h t", d=HD)).then_inc(stack_in[hq], 16)
                sp.dma_start(vs[hq][:, :, :, :].rearrange("p t h w -> p t (h w)"),
                             scratch["v"][hq][ds(S * b, S), :].rearrange("(t p) w -> p t w", p=P)).then_inc(v_in[hq], 16)

            def maxima_rows(n, hq):
                sp.wait_ge(max_split, n + 1)
                for j in range(3):
                    sp.dma_start(qs[hq][R_MAX + j:R_MAX + j + 1, :, :], mparts[:, hq % 2, j, :]).then_inc(mrow_in[hq], 16)

            def tile_rows(t, par):
                sp.dma_start(xrows[:, par], scratch["xn"].rearrange("(i p) d -> p i d", p=P)[:, ds(2 * t, 2), :]).then_inc(rows_in[par], 16)
                sp.dma_start(slots[:, par], keep["slot"][:, :, ds(2 * t, 2)]).then_inc(rows_in[par], 16)

            for hq in range(3):
                load(0, hq)
            for t in range(2):
                tile_rows(t, t)
            maxima_rows(0, 0)

            def body(t, b, hq, has):
                par = hq % 2
                if has(3):
                    sp.wait_ge(pv_done, PRING + NU * t)
                    load(*quad(b, hq, 3))
                if has(1):
                    maxima_rows(t + 1, (hq + 1) % NQ)
                sp.wait_ge(rows_out[par], 64 * (2 * b + hq // 2 + 1))
                if has(2):
                    tile_rows(t + 2, par)

            steps(sp, body)
            for i in range(2):
                sp.wait_ge(rows_out[i], 64 * (B * NQ // 2))

        @block.gpsimd
        def _(pool):
            def body(t, b, hq, has):
                par = hq % 2
                wait_apart(pool, rows_in[par], 32 * (2 * b + hq // 2 + 1))
                for i in range(2):
                    for k in range(2):
                        pool.indirect_dma_start(scratch["xs"], bass.IndirectOffsetOnAxis(ap=slots[:, par, k, i:i + 1].bitcast(U32), axis=0),
                                                xrows[:, par, i, :], None).then_inc(rows_out[par], 16)
                for j in range(1, NU + 1):
                    if j == NU and not has(1):
                        continue
                    mask_unit(NU * t + j, j % NU)

            def mask_unit(n, u):
                if not DIAG[u]:
                    return
                wait_apart(pool, exp_done, 4 * n + 4 + RING)
                for c in DIAG[u]:
                    part = probs[:, u % PRING, :, c:c + P]
                    pool.affine_select(out=part, in_=part, compare_op=ALU.is_ge, fill=0.0, base=0,
                                       pattern=[[0, 4], [1, P]], channel_multiplier=-1).then_inc(masked, 1)

            mask_unit(0, 0)
            steps(pool, body)

        @block.vector
        def _(dve):
            dve.sem_inc(m_taken, RING)
            dve.memset(cpsum[:, :, :], 0.0).then_inc(cleared, 1)

            def item(t, hq, k):
                n = NI * t + k
                slot = (NI * hq + k) % RING
                dve.wait_ge(m_taken, n + 1)
                wait_apart(dve, m_ready, n + 1)
                if k < NI - 1:
                    h, qt = ITEMS[k]
                    w = (qt + 1) * P
                    last = dve.tensor_tensor_reduce(junk[:, slot, 0:w], mpsum[:, slot, 0:w], keep["mask"][:, S - w:S], 1.0, 3 * NEG,
                                                    ALU.add, ALU.max, maxima[:, hq % 2, h, qt:qt + 1])
                    last.then_inc(m_taken, 1)
                    return
                mT = mpsum[0:4 * KT, slot, 0:P]
                parts = mparts[:, hq % 2]
                dve.tensor_scalar(parts[:, 0], mT, -1.0, None, ALU.mult).then_inc(max_step, 1)
                dve.wait_ge(max_step, 3 * t + 1)
                dve.scalar_tensor_tensor(mrest[:, :], mT, -1.0, parts[:, 0], ALU.mult, ALU.subtract).then_inc(m_taken, 1)
                dve.wait_ge(m_taken, n + 1 + RING)
                dve.tensor_copy(parts[:, 1], mrest[:, :]).then_inc(max_step, 1)
                dve.wait_ge(max_step, 3 * t + 2)
                dve.tensor_tensor(parts[:, 2], mrest[:, :], parts[:, 1], ALU.subtract).then_inc(max_step, 1)
                dve.wait_ge(max_step, 3 * t + 3)
                dve.sem_inc(max_split, 1)

            for k in range(NI):
                item(0, 0, k)
            for k in range(LEAD):
                item(1, 1, k)

            def body(t, b, hq, has):
                for slot in SLOT_ITEMS:
                    for j, k in slot:
                        if has(j):
                            item(t + j, (hq + j) % NQ, k)

            steps(dve, body)

        @block.scalar
        def _(act):
            act.sem_inc(exp_done, RING)

            def exps(n, u, heads):
                for h in heads:
                    m = 4 * n + h
                    act.wait_ge(s_ready, m + 1)
                    if h == 0:
                        act.wait_ge(pv_done, n + 1)
                    act.activation(probs[:, u % PRING, h], spsum[:, h % 2], ACT.Exp, scale=SCALE).then_inc(exp_done, 1)

            exps(0, 0, range(4))

            def body(t, b, hq, has):
                for u in range(1, NU):
                    exps(NU * t + u, u, range(4))
                if has(1):
                    exps(NU * t + NU, 0, range(4))
                act.wait_ge(pv_done, NU * t + NU + PRING)
                act.activation(keep["ctxT"][:, ds(t, 1), 0:CH].rearrange("p a c -> p (a c)"), cpsum[:, 0], ACT.Copy)
                act.activation(keep["ctxT"][:, ds(t, 1), CH:S].rearrange("p a c -> p (a c)"), cpsum[:, 1], ACT.Copy).then_inc(ctx_taken, 1)

            steps(act, body)

        @block.tensor
        def _(pe):
            pe.sem_inc(pv_done, PRING)
            pe.sem_inc(ctx_taken, 1)
            pe.wait_ge(cleared, 1)
            pe.wait_ge(const_in, 16 * 2 * NQ)

            def item(t, b, hq, k):
                n = NI * t + k
                slot = (NI * hq + k) % RING
                if k == 0:
                    pe.wait_ge(stack_in[hq], 16 * STACK_DMAS * (b + 1))
                pe.wait_ge(m_taken, n + 1)
                if k < NI - 1:
                    h, qt = ITEMS[k]
                    w = (qt + 1) * P
                    for c in range(0, w, CH):
                        e = min(w, c + CH)
                        last = pe.matmul(mpsum[:, slot, c:e], qs[hq][0:R_MAX, h, qt * P:(qt + 1) * P], ks[hq][0:R_MAX, h, c:e],
                                         start=True, stop=True)
                    last.then_inc(m_ready, 1)
                else:
                    pe.wait_ge(m_taken, n + RING)
                    pe.transpose(mpsum[0:4 * KT, slot, 0:P], maxima[:, hq % 2].rearrange("p h q -> p (h q)"), keep["ident"][:, :]).then_inc(m_ready, 1)

            def scores(n, hq, u, h):
                m = 4 * n + h
                pe.wait_ge(exp_done, m + 1)
                for c, kt, q0, w in UNITS[u]:
                    last = pe.matmul(spsum[:, h % 2, c:c + w], ks[hq][:, h, kt * P:(kt + 1) * P], qs[hq][:, h, q0:q0 + w],
                                     start=True, stop=True)
                last.then_inc(s_ready, 1)

            def weighted(n, t, b, hq, u):
                pe.wait_ge(exp_done, 4 * n + 4 + RING)
                if DIAG[u]:
                    pe.wait_ge(masked, MASKED[NU] * t + MASKED[u + 1])
                if u == 0:
                    pe.wait_ge(v_in[hq], 16 * (b + 1))
                    pe.wait_ge(ctx_taken, t + 1)
                for c, kt, q0, w in UNITS[u]:
                    half = q0 // CH
                    for h in range(4):
                        last = pe.matmul(cpsum[32 * h:32 * h + VW, half, q0 - half * CH:q0 - half * CH + w], vs[hq][:, kt, h], probs[:, u % PRING, h, c:c + w],
                                         start=kt == 0, stop=kt == (3 if half == 0 else 7), tile_position=(0, 32 * h), skip_group_check=True)
                last.then_inc(pv_done, 1)

            for k in range(NI):
                item(0, 0, 0, k)
            pe.wait_ge(mrow_in[0], 48)
            for k in range(LEAD):
                item(1, 0, 1, k)
                if k % 3 == 0:
                    scores(0, 0, 0, k // 3)

            def body(t, b, hq, has):
                for j in range(1, NU + 1):
                    u, n = j % NU, NU * t + j
                    b1, hq1 = quad(b, hq, 1) if j == NU else (b, hq)
                    for h in range(4):
                        if j < NU or has(1):
                            if u == 0 and h == 0:
                                pe.wait_ge(mrow_in[hq1], 48 * (b1 + 1))
                            scores(n, hq1, u, h)
                        for ahead, k in SLOT_ITEMS[4 * (j - 1) + h]:
                            if has(ahead):
                                item(t + ahead, *quad(b, hq, ahead), k)
                    weighted(n - 1, t, b, hq, j - 1)

            steps(pe, body)


def experts(nc, ins, scratch, keep):
    with ExitStack() as ctx:
        sb = lambda name, shape, dt=F32: ctx.enter_context(nc.sbuf_tensor(name, shape, dt))
        sem = lambda name: ctx.enter_context(nc.semaphore(name))
        w_gu = sb("w_gu", [P, NE * DH, 2 * HID])
        w_down = sb("w_down", [P, NE * DH, D])
        rows = sb("rows", [P, 2, D])
        xT = sb("xTs", [P, 2, DH, P])
        gate = sb("gate", [P, 2, HID])
        hid = sb("hid", [P, 2, HID])
        hT = sb("hT", [P, 2, DH, P])
        y = sb("y", [P, 2, D])
        tp = ctx.enter_context(nc.psum_tensor("tp", [P, 2, CH], F32))
        gu = ctx.enter_context(nc.psum_tensor("gu", [P, 2, CH], F32))
        hp = ctx.enter_context(nc.psum_tensor("hp", [P, 2, CH], F32))
        yp = ctx.enter_context(nc.psum_tensor("yp", [P, 2, CH], F32))
        w_in = sem("w_in")
        rows_in = [sem(f"srows_in{i}") for i in range(2)]
        y_out = [sem(f"y_out{i}") for i in range(2)]
        tp_ready, xT_ready = sem("tps_ready"), sem("xTs_ready")
        gu_ready, gate_ready, hid_ready = sem("gu_ready"), sem("gate_ready"), sem("hid_ready")
        hp_ready, hT_ready = sem("hp_ready"), sem("hT_ready")
        yp_ready, y_ready = sem("yp_ready"), sem("y_ready")
        block = ctx.enter_context(nc.Block())
        xs = scratch["xs"].rearrange("(s p) d -> s p d", p=P)
        ys = scratch["ys"].rearrange("(s p) d -> s p d", p=P)

        def tiles(eng, body):
            with eng.Fori(0, NST // 2) as i:
                for par in range(2):
                    body(2 * i + par, par, i)

        @block.sync
        def _(sp):
            for e in range(NE):
                sp.dma_start(w_gu[:, e * DH:(e + 1) * DH], ins["w_gu"][:, e * DH:(e + 1) * DH]).then_inc(w_in, 16)
                sp.dma_start(w_down[:, e * DH:(e + 1) * DH], ins["w_down"][:, e * DH:(e + 1) * DH]).then_inc(w_in, 16)
                if e == 0:
                    sp.sem_inc(tp_ready, 2)

            def body(s, par, i):
                sp.wait_ge(tp_ready, s + 1)
                sp.dma_start(rows[:, par], xs[ds(s, 1)].rearrange("a p d -> (a p) d")).then_inc(rows_in[par], 16)

            tiles(sp, body)

        @block.scalar
        def _(act):
            for i in range(2):
                act.sem_inc(y_out[i], 16)

            def xT_copy(s, par):
                act.wait_ge(tp_ready, s + 1 + 2)
                act.activation(xT[:, par].rearrange("p a t -> p (a t)"), tp[:, par, 0:D], ACT.Copy).then_inc(xT_ready, 1)

            def gelu(s, par):
                act.wait_ge(gu_ready, s + 1)
                act.activation(gate[:, par], gu[:, par, 0:HID], ACT.Gelu_apprx_tanh).then_inc(gate_ready, 1)

            def store(s, par, i):
                act.wait_ge(yp_ready, s + 1)
                act.wait_ge(y_out[par], 16 * (i + 1))
                act.activation(y[:, par], yp[:, par, 0:D], ACT.Copy).then_inc(y_ready, 1)
                act.wait_ge(y_ready, s + 1)
                act.dma_start(ys[ds(s, 1)].rearrange("a p d -> (a p) d"), y[:, par]).then_inc(y_out[par], 16)

            xT_copy(0, 0)
            gelu(0, 0)
            xT_copy(1, 1)
            with act.Fori(0, NST // 2 - 1) as i:
                for odd in (1, 0):
                    s = 2 * i + (1 if odd else 2)
                    gelu(s, odd)
                    xT_copy(s + 1, 1 - odd)
                    store(s - 1, 1 - odd, i)
            gelu(NST - 1, 1)
            store(NST - 2, 0, NST // 2 - 1)
            store(NST - 1, 1, NST // 2 - 1)
            for i in range(2):
                act.wait_ge(y_out[i], 16 + 16 * (NST // 2))

        @block.vector
        def _(dve):
            def body(s, par, i):
                dve.wait_ge(gate_ready, s + 1)
                dve.tensor_tensor(hid[:, par], gu[:, par, HID:2 * HID], gate[:, par], ALU.mult).then_inc(hid_ready, 1)
                dve.wait_ge(hp_ready, s + 1)
                dve.tensor_copy(hT[:, par].rearrange("p a t -> p (a t)"), hp[:, par, 0:HID]).then_inc(hT_ready, 1)

            tiles(dve, body)

        @block.tensor
        def _(pe):
            pe.wait_ge(w_in, 16 * 2 * NE)

            def rows_T(s, par, i):
                pe.wait_ge(rows_in[par], 16 * (i + 1))
                for dh in range(DH):
                    last = pe.transpose(tp[:, par, dh * P:(dh + 1) * P], rows[:, par, dh * P:(dh + 1) * P], keep["ident"][:, :])
                last.then_inc(tp_ready, 1)

            def gate_up(s, par):
                e = pe.value_load(keep["tile_expert"][0:1, ds(s, 1)], min_val=0, max_val=NE - 1)
                pe.wait_ge(xT_ready, s + 1)
                for dh in range(DH):
                    last = pe.matmul(gu[:, par], xT[:, par, dh], w_gu[:, ds(e * DH + dh, 1)].rearrange("p a c -> p (a c)"),
                                     start=dh == 0, stop=dh == DH - 1)
                last.then_inc(gu_ready, 1)

            def hidden_T(s, par):
                pe.wait_ge(hid_ready, s + 1)
                for dh in range(DH):
                    last = pe.transpose(hp[:, par, dh * P:(dh + 1) * P], hid[:, par, dh * P:(dh + 1) * P], keep["ident"][:, :])
                last.then_inc(hp_ready, 1)

            def down(s, par):
                e = pe.value_load(keep["tile_expert"][0:1, ds(s, 1)], min_val=0, max_val=NE - 1)
                pe.wait_ge(hT_ready, s + 1)
                for dh in range(DH):
                    last = pe.matmul(yp[:, par, 0:D], hT[:, par, dh], w_down[:, ds(e * DH + dh, 1)].rearrange("p a c -> p (a c)"),
                                     start=dh == 0, stop=dh == DH - 1)
                last.then_inc(yp_ready, 1)

            rows_T(0, 0, 0)
            gate_up(0, 0)
            rows_T(1, 1, 0)
            with pe.Fori(0, NST // 2 - 1) as i:
                for odd in (1, 0):
                    s = 2 * i + (1 if odd else 2)
                    gate_up(s, odd)
                    hidden_T(s - 1, 1 - odd)
                    rows_T(s + 1, 1 - odd, i + 1)
                    down(s - 1, 1 - odd)
            gate_up(NST - 1, 1)
            for s in (NST - 2, NST - 1):
                hidden_T(s, s % 2)
                down(s, s % 2)


def combine(nc, ins, scratch, keep, out):
    with ExitStack() as ctx:
        sb = lambda name, shape, dt=F32: ctx.enter_context(nc.sbuf_tensor(name, shape, dt))
        sem = lambda name: ctx.enter_context(nc.semaphore(name))
        w_o = sb("w_o", [P, NQ, D])
        sel = sb("sel", [P, P])
        bias = sb("bias", [P, D])
        inv = sb("inv", [P, 2, CH])
        ctxn = sb("ctxn", [P, NQ, S])
        xr = sb("xr", [P, 2, D])
        xb = sb("xb", [P, 2, D])
        yk = sb("yk", [P, 2, 2, D])
        slots = sb("slots_c", [P, 2, KT], I32)
        wts = sb("wts", [P, 2, KT])
        acc = sb("acc", [P, 2, 3, D])
        total = ctx.enter_context(nc.psum_tensor("total_ps", [P, 2, CH], F32))
        proj = ctx.enter_context(nc.psum_tensor("proj", [P, 2, CH], F32))
        w_in = sem("wo_in")
        passed = sem("passed5")
        x_in = [sem(f"xr_in{i}") for i in range(2)]
        slots_in = sem("slots_in")
        y_in = [sem(f"y_in{i}") for i in range(2)]
        out_done = [sem(f"out_done{i}") for i in range(2)]
        total_ready, inv_ready, norm_ready = sem("total_ready"), sem("inv_ready"), sem("norm_ready")
        proj_ready, xb_ready, acc_step, sum_ready = sem("proj_ready"), sem("xb_ready"), sem("acc_step"), sem("sum_ready")
        block = ctx.enter_context(nc.Block())
        x_rows = ins["x"].rearrange("(g p) d -> g p d", p=P)
        out_rows = out.rearrange("(g p) d -> g p d", p=P)
        HALVES = NQ * 2

        @block.sync
        def _(sp):
            sp.dma_start(w_o[:, :, :], ins["w_o"]).then_inc(w_in, 16)
            sp.dma_start(sel[:, :], ins["c_sel"]).then_inc(w_in, 16)
            sp.dma_start(bias[:, :], ins["bo"].partition_broadcast(P)).then_inc(w_in, 16)
            for i in range(2):
                sp.sem_inc(out_done[i], 16)
            sp.sem_inc(xb_ready, 2)
            sp.sem_inc(sum_ready, 2)

            def finished(g, par, b, i):
                sp.wait_ge(sum_ready, g + 1 + 2)
                sp.dma_start(out_rows[ds(g, 1)].rearrange("a p d -> (a p) d"), acc[:, par, 2]).then_inc(out_done[par], 16)

            with sp.Fori(0, B) as b:
                sp.wait_ge(sum_ready, KT * b + 2)
                sp.dma_start(slots[:, :, :], keep["slot"][:, :, ds(KT * b, KT)]).then_inc(slots_in, 16)
                sp.dma_start(wts[:, :, :], keep["weight"][:, :, ds(KT * b, KT)]).then_inc(slots_in, 16)
                for i in range(KT):
                    g, par = KT * b + i, i % 2
                    sp.wait_ge(xb_ready, g + 1)
                    sp.dma_start(xr[:, par], x_rows[ds(g, 1)].rearrange("a p d -> (a p) d")).then_inc(x_in[par], 16)
                    if i >= 1:
                        finished(g - 1, 1 - par, b, i)
                finished(KT * b + KT - 1, 1, b, KT)
            for i in range(2):
                sp.wait_ge(out_done[i], 16 + 16 * (NT // 2))

        @block.gpsimd
        def _(pool):
            pool.wait_ge(w_in, 48)
            with pool.Fori(0, B) as b:
                pool.wait_ge(slots_in, 32 * (b + 1))
                for i in range(KT):
                    g, par = KT * b + i, i % 2
                    pool.wait_ge(sum_ready, g + 1)
                    pool.sem_inc(passed, 1)
                    for k in range(2):
                        pool.indirect_dma_start(yk[:, par, k], None, scratch["ys"],
                                                bass.IndirectOffsetOnAxis(ap=slots[:, k, i:i + 1].bitcast(U32), axis=0)).then_inc(y_in[par], 16)
                    pool.wait_ge(x_in[par], 16 * (KT // 2 * b + i // 2 + 1))
                    pool.tensor_tensor(xb[:, par], xr[:, par], bias[:, :], ALU.add).then_inc(xb_ready, 1)

        @block.tensor
        def _(pe):
            pe.wait_ge(w_in, 48)
            pe.sem_inc(inv_ready, 2)
            with pe.Fori(0, B) as b:
                for j in range(HALVES):
                    n = HALVES * b + j
                    pe.wait_ge(inv_ready, n + 1)
                    pe.matmul(total[:, j % 2], sel[:, :], keep["ctxT"][:, ds(NQ * b + j // 2, 1), CH * (j % 2):CH * (j % 2 + 1)].rearrange("p a c -> p (a c)"),
                              start=True, stop=True).then_inc(total_ready, 1)
                pe.wait_ge(norm_ready, HALVES * b + HALVES)
                for i in range(KT):
                    g = KT * b + i
                    pe.wait_ge(sum_ready, g + 1)
                    for q in range(NQ):
                        last = pe.matmul(proj[:, i % 2, 0:D], ctxn[:, q, i * P:(i + 1) * P], w_o[:, q], start=q == 0, stop=q == NQ - 1)
                    last.then_inc(proj_ready, 1)

        @block.vector
        def _(dve):
            with dve.Fori(0, B) as b:
                dve.wait_ge(slots_in, 32 * (b + 1))
                for j in range(HALVES):
                    n = HALVES * b + j
                    dve.wait_ge(total_ready, n + 1)
                    dve.reciprocal(inv[:, j % 2], total[:, j % 2]).then_inc(inv_ready, 1)
                    dve.wait_ge(inv_ready, n + 1 + 2)
                    dve.tensor_tensor(ctxn[:, j // 2, CH * (j % 2):CH * (j % 2 + 1)], inv[:, j % 2],
                                      keep["ctxT"][:, ds(NQ * b + j // 2, 1), CH * (j % 2):CH * (j % 2 + 1)].rearrange("p a c -> p (a c)"),
                                      ALU.mult).then_inc(norm_ready, 1)
                for i in range(KT):
                    g, par = KT * b + i, i % 2
                    dve.wait_ge(proj_ready, g + 1)
                    dve.wait_ge(xb_ready, g + 1 + 2)
                    dve.tensor_tensor(acc[:, par, 0], proj[:, par, 0:D], xb[:, par], ALU.add).then_inc(acc_step, 1)
                    dve.wait_ge(acc_step, 2 * g + 1)
                    dve.wait_ge(y_in[par], 32 * (KT // 2 * b + i // 2 + 1))
                    dve.scalar_tensor_tensor(acc[:, par, 1], yk[:, par, 0], wts[:, 0, i:i + 1], acc[:, par, 0], ALU.mult, ALU.add).then_inc(acc_step, 1)
                    dve.wait_ge(acc_step, 2 * g + 2)
                    dve.wait_ge(out_done[par], 16 * (KT // 2 * b + i // 2 + 1))
                    dve.scalar_tensor_tensor(acc[:, par, 2], yk[:, par, 1], wts[:, 1, i:i + 1], acc[:, par, 1], ALU.mult, ALU.add).then_inc(sum_ready, 1)


def build(nc, ins, out):
    with ExitStack() as ctx:
        sb = lambda name, shape, dt=F32: ctx.enter_context(nc.sbuf_tensor(name, shape, dt))
        keep = {
            "ident": sb("ident", [P, P]),
            "mhalf": sb("mhalf", [P, NT]),
            "mask": sb("mask", [P, S]),
            "msq": sb("msq", [P, NT]),
            "logits": sb("logits", [P, NT, NE]),
            "weight": sb("weight", [P, 2, NT]),
            "slot": sb("slot", [P, 2, NT], I32),
            "tile_expert": sb("tile_expert", [1, NST], I32),
            "ctxT": sb("ctxT", [P, B * NQ, S]),
        }
        scratch = {
            "xn": nc.dram_tensor("xn_rows", [TOK, D], F32).ap(),
            "qk": nc.dram_tensor("qk_parts", [NQ, 3, P, TOK], BF16).ap(),
            "v": nc.dram_tensor("v_rows", [NQ, TOK, 4 * VW], F32).ap(),
            "xs": nc.dram_tensor("slot_rows", [NST * P, D], F32).ap(),
            "ys": nc.dram_tensor("expert_rows", [NST * P, D], F32).ap(),
        }
        project(nc, ins, scratch, keep)
        route(nc, ins, scratch, keep)
        attend(nc, ins, scratch, keep)
        experts(nc, ins, scratch, keep)
        combine(nc, ins, scratch, keep, out)


def bf16_bits(a):
    bits = np.asarray(a, np.float32).view(np.uint32)
    return (bits >> 16).astype(np.uint16)


def constants():
    slopes = (2.0 ** (-8.0 * np.arange(1, NH + 1) / NH)).astype(np.float32)
    parts, rest = [], slopes.copy()
    for _ in range(3):
        top = (rest.view(np.uint32) & np.uint32(0xFFFF0000)).view(np.float32)
        parts.append(top)
        rest = rest - top
    c_q = np.zeros((NQ, 6, 4, S), np.float32)
    for j in range(6):
        c_q[:, j] = parts[j % 3].reshape(NQ, 4, 1)
    pos = np.arange(S)
    c_k = np.ones((9, 4, S), np.float32)
    c_k[0:3] = (pos // 256 * 256)[None, None, :]
    c_k[3:6] = (pos % 256)[None, None, :]
    c_sel = np.zeros((P, P), np.float32)
    for h in range(4):
        c_sel[32 * h + HD, 32 * h:32 * h + 32] = 1.0
    return bf16_bits(c_q), bf16_bits(c_k), c_sel


def kernel(L0_attn_x, L0_attn_Wq, L0_attn_Wk, L0_attn_Wv, L0_attn_Wo, L0_attn_bo, L0_ffn_router_logits,
           L0_ffn_gating_einsum, L0_ffn_linear, L0_ffn_per_expert_scale, L0_ffn_router_scale):
    import concourse.bacc as bacc
    from concourse.bass_utils import run_bass_kernel_spmd

    split = lambda w: np.asarray(w).reshape(DH, P, -1).transpose(1, 0, 2)
    wq, wk = (split(w).reshape(P, DH, NQ, 4 * HD) for w in (L0_attn_Wq, L0_attn_Wk))
    w_o = np.zeros((NQ, 4, 32, D), np.float32)
    w_o[:, :, 0:HD] = np.asarray(L0_attn_Wo).reshape(NQ, 4, HD, D)
    w_gu = np.asarray(L0_ffn_gating_einsum).reshape(NE, 2 * HID, DH, P).transpose(3, 0, 2, 1)
    w_down = np.asarray(L0_ffn_linear).reshape(NE, DH, P, D).transpose(2, 0, 1, 3)
    c_q, c_k, c_sel = constants()
    arrays = {
        "x": np.asarray(L0_attn_x).reshape(TOK, D),
        "w_qk": np.concatenate([wq, wk], axis=3),
        "w_v": split(L0_attn_Wv),
        "w_r": split(L0_ffn_router_logits),
        "router_scale": np.asarray(L0_ffn_router_scale).reshape(DH, P).T,
        "w_o": w_o.reshape(NQ, P, D).transpose(1, 0, 2),
        "bo": np.asarray(L0_attn_bo),
        "w_gu": w_gu.reshape(P, NE * DH, 2 * HID),
        "w_down": w_down.reshape(P, NE * DH, D),
        "expert_scale": np.asarray(L0_ffn_per_expert_scale),
        "c_q": c_q,
        "c_k": c_k,
        "c_sel": c_sel,
    }
    arrays = {"in_" + k: np.ascontiguousarray(v) for k, v in arrays.items()}
    nc = bacc.Bacc("TRN2", target_bir_lowering=False, num_devices=1)
    ins = {}
    for name, a in arrays.items():
        ap = nc.dram_tensor(name, a.shape, mybir.dt.from_np(a.dtype), kind="ExternalInput").ap()
        ins[name[3:]] = ap.bitcast(BF16) if a.dtype == np.uint16 else ap
    out = nc.dram_tensor("out", (TOK, D), F32, kind="ExternalOutput").ap()
    build(nc, ins, out)
    r = run_bass_kernel_spmd(nc, [arrays], core_ids=[0])
    return r.results[0]["out"].reshape(B, S, D)
```

```python
from contextlib import ExitStack

import concourse.bass as bass
from concourse import mybir
import numpy as np

P = 128
F32 = mybir.dt.float32
BF16 = mybir.dt.bfloat16
I32 = mybir.dt.int32
U32 = mybir.dt.uint32
U16 = mybir.dt.uint16
ALU = mybir.AluOpType
ACT = mybir.ActivationFunctionType
AX_X = mybir.AxisListType.X
ds = bass.ds

B, S, D = 4, 1024, 256
NH, HD = 16, 16
TOK = B * S
NT = TOK // P
DH = D // P
NQ = NH // 4
NE, HID = 8, 256
CH = 512
NC = TOK // CH
NST = 2 * TOK // P + NE
LN_EPS, RMS_EPS = 1e-5, 1e-6
NEG = -1e30
KT = S // P

Q_PART = [0, 1, 2, 0, 1, 0]
K_PART = [0, 0, 0, 1, 1, 2]
R_ALIBI = 6 * HD
R_MAX = R_ALIBI + 6
ROWS = R_MAX + 3
VW = HD + 1
SCALE = float(HD) ** -0.5

UNITS = [
    [(0, 0, 0, 512)],
    [(0, 0, 512, 512)],
    [(0, 1, 128, 384), (384, 3, 384, 128)],
    [(0, 1, 512, 512)],
    [(0, 2, 256, 256), (256, 6, 768, 256)],
    [(0, 2, 512, 512)],
    [(0, 3, 512, 512)],
    [(0, 4, 512, 512)],
    [(0, 5, 640, 384), (384, 7, 896, 128)],
]
NU = len(UNITS)
DIAG = [[c for c, kt, q0, _ in u if q0 == kt * P] for u in UNITS]
MASKED = [sum(map(len, DIAG[:u])) for u in range(NU + 1)]
PRING = 3

ITEMS = [(h, qt) for h in range(4) for qt in (7, 0, 6, 1, 5, 2, 4, 3)]
NI = len(ITEMS) + 1
LEAD = 12
SLOTS = 4 * NU
FIRST_PART = 24


def slot_items():
    ahead1 = [(1, k) for k in range(LEAD, NI)]
    ahead2 = [(2, k) for k in range(LEAD)]
    out, done = [], 0
    for s in range(SLOTS):
        if s < FIRST_PART:
            upto = (s + 1) * len(ahead1) // FIRST_PART
            out.append(ahead1[done:upto])
            done = upto
        else:
            n = s - FIRST_PART
            out.append(ahead2[n:n + 1])
    return out


SLOT_ITEMS = slot_items()
assert sum(map(len, SLOT_ITEMS)) == NI


def project(nc, ins, scratch, keep):
    with ExitStack() as ctx:
        sb = lambda name, shape, dt=F32: ctx.enter_context(nc.sbuf_tensor(name, shape, dt))
        ps = lambda name, shape: ctx.enter_context(nc.psum_tensor(name, shape, F32))
        sem = lambda name: ctx.enter_context(nc.semaphore(name))
        w_qk = sb("w_qk", [P, DH, NQ, P])
        w_vr = sb("w_vr", [P, DH, D + NE])
        rscale = sb("rscale", [P, DH])
        ident, mhalf = keep["ident"], keep["mhalf"]
        x_in = sb("x_in", [P, 2, 4, D])
        xn = sb("xn", [P, 2, 4, D])
        stats = sb("stats", [P, 2, 4, 6])
        mv = sb("mv", [P, 2, 4, 2])
        veps = sb("veps", [P, 2, 4])
        rstd = sb("rstd", [P, 2, 4])
        rsq = sb("rsq", [P, 2, 4])
        xT = sb("xT", [P, 2, DH, CH])
        rest = sb("rest", [P, 2, CH])
        parts = sb("parts", [P, NQ, 3, CH], BF16)
        vt = sb("vt", [P, 2, 4, NQ, 4, VW])
        zeros = sb("zeros", [P, 2048])
        tpsum = ps("tpsum", [P, DH, CH])
        qkpsum = ps("qkpsum", [P, 2, CH])
        vpsum = ps("vpsum", [P, 2, CH])

        weights_in = sem("weights_in")
        zeros_set = sem("zeros_set")
        const_set = sem("const_set")
        rweight_set = sem("rweight_set")
        ones_set = sem("ones_set")
        passed = sem("passed1")
        x_loaded = [sem(f"x_loaded{i}") for i in range(2)]
        x_stored = [sem(f"x_stored{i}") for i in range(2)]
        parts_stored = [sem(f"parts_stored{i}") for i in range(NQ)]
        v_stored = [sem(f"v_stored{i}") for i in range(2)]
        zeros_stored = sem("zeros_stored")
        dve_step = sem("dve_step")
        pool_step = sem("pool_step")
        mv_ready = sem("mv_ready")
        rstd_ready = sem("rstd_ready")
        xn_ready = sem("xn_ready")
        tp_ready = sem("tp_ready")
        xT0_ready = sem("xT0_ready")
        xT1_ready = sem("xT1_ready")
        qk_ready = sem("qk_ready")
        p1_ready = sem("p1_ready")
        rest_ready = sem("rest_ready")
        p2_ready = sem("p2_ready")
        p3_ready = sem("p3_ready")
        v_ready = sem("v_ready")
        v_taken = sem("v_taken")
        block = ctx.enter_context(nc.Block())

        RING = 2

        def chunks(eng, body):
            with eng.Fori(0, NC // 2 - 1) as i:
                body(2 * i, 0, True, i)
                body(2 * i + 1, 1, True, i)
            body(NC - 2, 0, True, NC // 2 - 1)
            body(NC - 1, 1, False, NC // 2 - 1)

        x_rows = ins["x"].rearrange("(c t p) d -> c p t d", c=NC, p=P)
        xn_rows = scratch["xn"].rearrange("(c t p) d -> c p t d", c=NC, p=P)
        n_zero = NST * P * D // (P * 2048)

        @block.sync
        def _(sp):
            for i in range(2):
                sp.sem_inc(x_stored[i], 16)
                sp.sem_inc(v_stored[i], 16 * NQ)
                sp.dma_start(x_in[:, i], x_rows[i]).then_inc(x_loaded[i], 16)
            for q in range(NQ):
                sp.sem_inc(parts_stored[q], 16)
            sp.dma_start(w_vr[:, :, 0:D], ins["w_v"]).then_inc(weights_in, 16)
            sp.dma_start(w_vr[:, :, D:D + NE], ins["w_r"]).then_inc(weights_in, 16)
            sp.dma_start(rscale[:, :], ins["router_scale"]).then_inc(weights_in, 16)
            sp.dma_start(w_qk[:, :, :, :], ins["w_qk"]).then_inc(weights_in, 16)

            def stores(c, par, load):
                sp.wait_ge(xn_ready, c + 1)
                sp.dma_start(xn_rows[ds(c, 1)].rearrange("a p t d -> (a p) t d"), xn[:, par]).then_inc(x_stored[par], 16)
                if load:
                    sp.dma_start(x_in[:, par], x_rows[ds(c + 2, 1)].rearrange("a p t d -> (a p) t d")).then_inc(x_loaded[par], 16)
                for q in range(NQ):
                    sp.wait_ge(p3_ready, 4 * c + q + 1 + RING)
                    sp.dma_start(scratch["qk"][q].rearrange("a p t -> p a t")[:, :, ds(CH * c, CH)],
                                 parts[:, q]).then_inc(parts_stored[q], 16)
                sp.wait_ge(v_taken, 4 * c + 4 + RING)
                for q in range(NQ):
                    sp.dma_start(scratch["v"][q].rearrange("(t p) w -> p t w", p=P)[:, ds(4 * c, 4), :],
                                 vt[:, par, :, q].rearrange("p t h w -> p t (h w)")).then_inc(v_stored[par], 16)

            with sp.Fori(0, NC // 2 - 1) as i:
                stores(2 * i, 0, True)
                stores(2 * i + 1, 1, True)
            sp.wait_ge(zeros_set, 1)
            flat = scratch["xs"].rearrange("(n p r) d -> n p (r d)", n=n_zero, p=P)
            for j in range(n_zero):
                sp.dma_start(flat[j], zeros[:, :]).then_inc(zeros_stored, 16)
            stores(NC - 2, 0, False)
            stores(NC - 1, 1, False)
            for i in range(2):
                sp.wait_ge(x_stored[i], 16 + 16 * (NC // 2))
                sp.wait_ge(v_stored[i], 16 * NQ * (1 + NC // 2))
            for q in range(NQ):
                sp.wait_ge(parts_stored[q], 16 + 16 * NC)
            sp.wait_ge(zeros_stored, 16 * n_zero)

        @block.gpsimd
        def _(pool):
            pool.sem_inc(p3_ready, RING)
            pool.memset(ident[:, :], 0.0).then_inc(pool_step, 1)
            pool.memset(mhalf[:, :], -0.5).then_inc(const_set, 1)
            pool.wait_ge(pool_step, 1)
            pool.affine_select(out=ident[:, :], in_=ident[:, :], compare_op=ALU.not_equal, fill=1.0,
                               base=0, pattern=[[-1, P]], channel_multiplier=1).then_inc(const_set, 1)
            pool.memset(vt[:, :, :, :, :, :].rearrange("p b t q h w -> p (b t q h) w")[:, :, HD:VW], 1.0).then_inc(ones_set, 1)
            pool.wait_ge(const_set, 2)
            STEPS = 3

            def rstds(c, par):
                k = 1 + STEPS * c
                pool.wait_ge(mv_ready, c + 1)
                pool.sem_inc(passed, 1)
                pool.tensor_scalar(veps[:, par], mv[:, par, :, 1], LN_EPS, None, ALU.add).then_inc(pool_step, 1)
                pool.wait_ge(pool_step, k + 1)
                pool.tensor_tensor(rstd[:, par], veps[:, par], mhalf[:, 0:4], ALU.pow).then_inc(rstd_ready, 1)
                pool.wait_ge(rstd_ready, c + 1)
                pool.tensor_tensor(rsq[:, par], rstd[:, par], rstd[:, par], ALU.mult).then_inc(pool_step, 1)
                pool.wait_ge(pool_step, k + 2)
                pool.tensor_tensor(keep["msq"][:, ds(4 * c, 4)], rsq[:, par], mv[:, par, :, 1], ALU.mult).then_inc(pool_step, 1)

            rstds(0, 0)
            pool.memset(zeros[:, :], 0.0).then_inc(zeros_set, 1)

            def body(c, par, nxt, i):
                if nxt:
                    rstds(c + 1, 1 - par)
                for q in range(NQ):
                    pool.wait_ge(p2_ready, 4 * c + q + 1)
                    pool.tensor_tensor(parts[:, q, 2], rest[:, q % 2], parts[:, q, 1], ALU.subtract).then_inc(p3_ready, 1)

            chunks(pool, body)

        @block.vector
        def _(dve):
            dve.sem_inc(rest_ready, RING)
            dve.wait_ge(weights_in, 64)
            for dh in range(DH):
                last = dve.tensor_scalar(w_vr[:, dh, D:D + NE], w_vr[:, dh, D:D + NE], rscale[:, dh:dh + 1], None, ALU.mult)
            last.then_inc(rweight_set, 1)

            def normalise(c, par, i):
                dve.wait_ge(x_loaded[par], 16 * (i + 1))
                for t in range(4):
                    last = dve.bn_stats(stats[:, par, t], x_in[:, par, t])
                last.then_inc(dve_step, 1)
                dve.wait_ge(dve_step, c + 1)
                dve.sem_inc(passed, 1)
                for t in range(4):
                    last = dve.bn_aggr(mv[:, par, t], stats[:, par, t])
                last.then_inc(mv_ready, 1)
                dve.wait_ge(mv_ready, c + 1)
                dve.wait_ge(rstd_ready, c + 1)
                dve.wait_ge(x_stored[par], 16 * (i + 1))
                for t in range(4):
                    last = dve.tensor_scalar(xn[:, par, t], x_in[:, par, t], mv[:, par, t, 0:1],
                                             rstd[:, par, t:t + 1], ALU.subtract, ALU.mult)
                last.then_inc(xn_ready, 1)

            def evacuate(c, par):
                dve.wait_ge(tp_ready, 2 * c + 2)
                dve.tensor_copy(xT[:, par, 1], tpsum[:, 1]).then_inc(xT1_ready, 1)

            normalise(0, 0, 0)
            evacuate(0, 0)

            def body(c, par, nxt, i):
                if nxt:
                    normalise(c + 1, 1 - par, i + par)
                for q in range(NQ):
                    n = 4 * c + q
                    dve.wait_ge(p1_ready, n + 1)
                    dve.wait_ge(p3_ready, n + 1)
                    dve.tensor_tensor(rest[:, q % 2], qkpsum[:, q % 2], parts[:, q, 0], ALU.subtract).then_inc(rest_ready, 1)
                    dve.wait_ge(rest_ready, n + 1 + RING)
                    dve.tensor_copy(parts[:, q, 1], rest[:, q % 2]).then_inc(p2_ready, 1)
                if nxt:
                    evacuate(c + 1, 1 - par)

            chunks(dve, body)

        @block.scalar
        def _(act):
            act.sem_inc(v_taken, RING)

            def evacuate(c, par):
                act.wait_ge(tp_ready, 2 * c + 1)
                act.activation(xT[:, par, 0], tpsum[:, 0], ACT.Copy).then_inc(xT0_ready, 1)

            evacuate(0, 0)
            act.wait_ge(ones_set, 1)

            def body(c, par, nxt, i):
                for q in range(NQ):
                    n = 4 * c + q
                    act.wait_ge(qk_ready, n + 1)
                    act.wait_ge(parts_stored[q], 16 * (c + 1))
                    act.activation(parts[:, q, 0], qkpsum[:, q % 2], ACT.Copy).then_inc(p1_ready, 1)
                if nxt:
                    evacuate(c + 1, 1 - par)
                act.wait_ge(v_stored[par], 16 * NQ * (i + 1))
                for t in range(4):
                    act.wait_ge(v_ready, 4 * c + t + 1)
                    act.activation(vt[:, par, t].rearrange("p q h w -> p (q h) w")[:, :, 0:HD],
                                   vpsum[:, t % 2, 0:D].rearrange("p (g w) -> p g w", w=HD), ACT.Copy)
                    act.activation(keep["logits"][:, ds(4 * c + t, 1), :].rearrange("p a e -> p (a e)"),
                                   vpsum[:, t % 2, D:D + NE], ACT.Copy).then_inc(v_taken, 1)

            chunks(act, body)

        @block.tensor
        def _(pe):
            pe.wait_ge(const_set, 2)

            def transposes(c, par):
                pe.wait_ge(xn_ready, c + 1)
                for dh in range(DH):
                    for t in range(4):
                        last = pe.transpose(tpsum[:, dh, t * P:(t + 1) * P], xn[:, par, t, dh * P:(dh + 1) * P], ident[:, :])
                    last.then_inc(tp_ready, 1)

            transposes(0, 0)
            pe.wait_ge(weights_in, 64)
            pe.wait_ge(rweight_set, 1)

            def body(c, par, nxt, i):
                pe.wait_ge(xT0_ready, c + 1)
                pe.wait_ge(xT1_ready, c + 1)
                for q in range(NQ):
                    pe.wait_ge(rest_ready, 4 * c + q + 1)
                    for dh in range(DH):
                        last = pe.matmul(qkpsum[:, q % 2], w_qk[:, dh, q], xT[:, par, dh], start=dh == 0, stop=dh == DH - 1)
                    last.then_inc(qk_ready, 1)
                if nxt:
                    transposes(c + 1, 1 - par)
                for t in range(4):
                    pe.wait_ge(v_taken, 4 * c + t + 1)
                    for dh in range(DH):
                        last = pe.matmul(vpsum[:, t % 2, 0:D + NE], xT[:, par, dh, t * P:(t + 1) * P], w_vr[:, dh],
                                         start=dh == 0, stop=dh == DH - 1)
                    last.then_inc(v_ready, 1)

            chunks(pe, body)


def route(nc, ins, scratch, keep):
    with ExitStack() as ctx:
        sb = lambda name, shape, dt=F32: ctx.enter_context(nc.sbuf_tensor(name, shape, dt))
        sem = lambda name: ctx.enter_context(nc.semaphore(name))
        counts = ctx.enter_context(nc.psum_tensor("counts", [P, 2, CH], F32))
        E3 = [P, NT, NE]
        msqe, rms = sb("msqe", [P, NT]), sb("rms", [P, NT])
        logit = sb("logit", E3)
        top = [sb(f"top{k}", [P, NT]) for k in range(2)]
        hit, key = sb("hit", E3), sb("key", E3)
        first = sb("first", [P, NT])
        chosen = [sb(f"chosen{k}", E3) for k in range(2)]
        masked = sb("masked", E3)
        expd, prob = sb("expd", E3), sb("prob", E3)
        esum = sb("esum", [P, NT])
        picked = sb("picked", E3)
        pk = [sb(f"pk{k}", [P, NT]) for k in range(2)]
        renorm, guard = sb("renorm", [P, NT]), sb("guard", [P, NT])
        escale = sb("escale", [P, NE])
        sk = sb("sk", [P, NT])
        rank_of, reset = sb("rank_of", [P, NE]), sb("reset", [P, NE, NT])
        both = sb("both", E3, BF16)
        tri, ones = sb("tri", [P, P], BF16), sb("ones", [P, P], BF16)
        cnt, run = sb("cnt", [P, NE, NT]), sb("run", [P, NE, NT])
        pos = sb("pos", [P, NE, NT])
        total, total_i = sb("total", [P, NE]), sb("total_i", [P, NE], I32)
        tiles_i, tiles = sb("tiles_i", [P, NE], I32), sb("tiles", [P, NE])
        ends, base = sb("ends", [P, NE]), sb("base", [P, NE])
        slot_f = sb("slot_f", [P, NT])
        tile_no, past = sb("tile_no", [1, NST, NE]), sb("past", [1, NST, NE])
        tile_f = sb("tile_f", [1, NST])
        scale_in = sem("scale_in")
        pool_set = sem("pool_set")
        rms_ready = sem("rms_ready")
        pool_step = sem("pool_step_r")
        dve_step = sem("dve_step_r")
        shifted = sem("shifted")
        exp_ready = sem("exp_ready")
        both_ready = sem("both_ready")
        counted = sem("counted")
        routed = sem("routed")
        block = ctx.enter_context(nc.Block())
        per_expert = lambda a: a.rearrange("p (t a) -> p t a", a=1).to_broadcast(E3)

        @block.sync
        def _(sp):
            sp.dma_start(escale[:, :], ins["expert_scale"].partition_broadcast(P)).then_inc(scale_in, 16)
            sp.wait_ge(scale_in, 16)

        @block.gpsimd
        def _(pool):
            pool.tensor_scalar(msqe[:, :], keep["msq"][:, :], RMS_EPS, None, ALU.add).then_inc(pool_step, 1)
            pool.wait_ge(pool_step, 1)
            pool.tensor_tensor(rms[:, :], msqe[:, :], keep["mhalf"][:, 0:NT], ALU.pow).then_inc(rms_ready, 1)
            pool.iota(rank_of[:, :], pattern=[[-1, NE]], base=NE, channel_multiplier=0, allow_small_or_imprecise_dtypes=True).then_inc(pool_set, 1)
            pool.iota(tile_no[:, :, :], pattern=[[1, NST], [0, NE]], base=0, channel_multiplier=0, allow_small_or_imprecise_dtypes=True).then_inc(pool_set, 1)
            pool.memset(reset[:, :, :], 1.0).then_inc(pool_step, 1)
            pool.memset(ones[:, :], 1.0).then_inc(pool_set, 1)
            pool.wait_ge(pool_step, 2)
            pool.memset(reset[:, :, 0:1], 0.0).then_inc(pool_set, 1)
            pool.wait_ge(pool_set, 4)
            pool.affine_select(out=tri[:, :], in_=ones[:, :], compare_op=ALU.is_gt, fill=0.0,
                               base=0, pattern=[[1, P]], channel_multiplier=-1).then_inc(pool_set, 1)
            mask = keep["mask"]
            pool.memset(mask[:, :], 0.0).then_inc(pool_step, 1)
            pool.wait_ge(pool_step, 3)
            pool.affine_select(out=mask[:, :], in_=mask[:, :], compare_op=ALU.is_ge, fill=NEG,
                               base=S - P, pattern=[[-1, S]], channel_multiplier=1).then_inc(pool_set, 1)

        @block.tensor
        def _(pe):
            pe.wait_ge(pool_set, 5)
            pe.wait_ge(both_ready, 1)
            rhs = both[:, :, :].rearrange("p t e -> p (t e)")
            pe.matmul(counts[:, 0, 0:NT * NE], tri[:, :], rhs, start=True, stop=True)
            pe.matmul(counts[:, 1, 0:NT * NE], ones[:, :], rhs, start=True, stop=True).then_inc(counted, 1)

        @block.scalar
        def _(act):
            act.wait_ge(shifted, 1)
            act.activation(expd[:, :, :], expd[:, :, :], ACT.Exp).then_inc(exp_ready, 1)

        @block.vector
        def _(dve):
            steps = [0]

            def then(ins_):
                ins_.then_inc(dve_step, 1)
                steps[0] += 1
                dve.wait_ge(dve_step, steps[0])

            dve.wait_ge(rms_ready, 1)
            dve.wait_ge(pool_set, 6)
            dve.wait_ge(scale_in, 16)
            then(dve.tensor_scalar(rms[:, :], rms[:, :], float(D) ** -0.5, None, ALU.mult))
            then(dve.tensor_tensor(logit[:, :, :], keep["logits"][:, :, :], per_expert(rms[:, :]), ALU.mult))
            src = logit
            rank3 = rank_of[:, :].rearrange("p (a e) -> p a e", a=1).to_broadcast(E3)
            for k in range(2):
                then(dve.tensor_reduce(top[k][:, :], src[:, :, :], AX_X, ALU.max))
                then(dve.tensor_tensor(hit[:, :, :], src[:, :, :], per_expert(top[k][:, :]), ALU.is_equal))
                then(dve.tensor_tensor(key[:, :, :], hit[:, :, :], rank3, ALU.mult))
                then(dve.tensor_reduce(first[:, :], key[:, :, :], AX_X, ALU.max))
                then(dve.tensor_tensor(chosen[k][:, :, :], rank3, per_expert(first[:, :]), ALU.is_equal))
                if k == 0:
                    then(dve.scalar_tensor_tensor(masked[:, :, :].rearrange("p t e -> p (t e)"),
                                                  chosen[0][:, :, :].rearrange("p t e -> p (t e)"), NEG,
                                                  logit[:, :, :].rearrange("p t e -> p (t e)"), ALU.mult, ALU.add))
                    src = masked
            dve.tensor_tensor(expd[:, :, :], logit[:, :, :], per_expert(top[0][:, :]), ALU.subtract).then_inc(shifted, 1)
            dve.tensor_tensor(both[:, :, :], chosen[0][:, :, :], chosen[1][:, :, :], ALU.add).then_inc(both_ready, 1)
            dve.wait_ge(exp_ready, 1)
            then(dve.tensor_reduce(esum[:, :], expd[:, :, :], AX_X, ALU.add))
            then(dve.reciprocal(esum[:, :], esum[:, :]))
            then(dve.tensor_tensor(prob[:, :, :], expd[:, :, :], per_expert(esum[:, :]), ALU.mult))
            for k in range(2):
                then(dve.tensor_tensor(picked[:, :, :], prob[:, :, :], chosen[k][:, :, :], ALU.mult))
                then(dve.tensor_reduce(pk[k][:, :], picked[:, :, :], AX_X, ALU.add))
            then(dve.tensor_tensor(renorm[:, :], pk[0][:, :], pk[1][:, :], ALU.add))
            then(dve.tensor_scalar(guard[:, :], renorm[:, :], 0.0, None, ALU.is_le))
            then(dve.tensor_tensor(renorm[:, :], renorm[:, :], guard[:, :], ALU.add))
            then(dve.reciprocal(renorm[:, :], renorm[:, :]))
            scale3 = escale[:, :].rearrange("p (a e) -> p a e", a=1).to_broadcast(E3)
            for k in range(2):
                then(dve.tensor_tensor(picked[:, :, :], scale3, chosen[k][:, :, :], ALU.mult))
                then(dve.tensor_reduce(sk[:, :], picked[:, :, :], AX_X, ALU.add))
                then(dve.tensor_tensor(sk[:, :], sk[:, :], renorm[:, :], ALU.mult))
                then(dve.tensor_tensor(keep["weight"][:, k], sk[:, :], pk[k][:, :], ALU.mult))
            dve.wait_ge(counted, 1)
            view = lambda j: counts[:, j, 0:NT * NE].rearrange("p (t e) -> p e t", e=NE)
            then(dve.tensor_copy(cnt[:, :, :], view(1)))
            flat = lambda a: a[:, :, :].rearrange("p e t -> p (e t)")
            then(dve.tensor_tensor_scan(flat(run), flat(reset), flat(cnt), 0.0, ALU.mult, ALU.add))
            then(dve.tensor_scalar(total[:, :], run[:, :, NT - 1], float(P - 1), None, ALU.add))
            then(dve.tensor_copy(total_i[:, :], total[:, :]))
            then(dve.tensor_scalar(tiles_i[:, :], total_i[:, :], P.bit_length() - 1, None, ALU.arith_shift_right))
            then(dve.tensor_copy(tiles[:, :], tiles_i[:, :]))
            then(dve.tensor_tensor_scan(ends[:, :], reset[:, 0, 1:NE + 1], tiles[:, :], 0.0, ALU.mult, ALU.add))
            then(dve.tensor_tensor(base[:, :], ends[:, :], tiles[:, :], ALU.subtract))
            then(dve.tensor_scalar(base[:, :], base[:, :], float(P), None, ALU.mult))
            then(dve.tensor_tensor(pos[:, :, :], run[:, :, :], cnt[:, :, :], ALU.subtract))
            then(dve.tensor_tensor(pos[:, :, :], pos[:, :, :], view(0), ALU.add))
            then(dve.tensor_tensor(pos[:, :, :], pos[:, :, :], base[:, :].rearrange("p (e a) -> p e a", a=1).to_broadcast([P, NE, NT]), ALU.add))
            for k in range(2):
                then(dve.tensor_tensor(picked[:, :, :], pos[:, :, :].rearrange("p e t -> p t e"), chosen[k][:, :, :], ALU.mult))
                then(dve.tensor_reduce(slot_f[:, :], picked[:, :, :], AX_X, ALU.add))
                then(dve.tensor_copy(keep["slot"][:, k], slot_f[:, :]))
            then(dve.tensor_tensor(past[:, :, :], tile_no[:, :, :], ends[0:1, :].rearrange("p (a e) -> p a e", a=1).to_broadcast([1, NST, NE]), ALU.is_ge))
            then(dve.tensor_reduce(tile_f[:, :], past[:, :, :], AX_X, ALU.add))
            dve.tensor_scalar(keep["tile_expert"][:, :], tile_f[:, :], float(NE - 1), None, ALU.min).then_inc(routed, 1)
            dve.wait_ge(routed, 1)


def attend(nc, ins, scratch, keep):
    with ExitStack() as ctx:
        sb = lambda name, shape, dt=F32: ctx.enter_context(nc.sbuf_tensor(name, shape, dt))
        sem = lambda name: ctx.enter_context(nc.semaphore(name))
        qs = [sb(f"qs{i}", [ROWS, 4, S], BF16) for i in range(NQ)]
        ks = [sb(f"ks{i}", [ROWS, 4, S], BF16) for i in range(NQ)]
        vs = [sb(f"vs{i}", [P, KT, 4, VW]) for i in range(NQ)]
        probs = sb("probs", [P, PRING, 4, CH])
        junk = sb("junk", [P, 2, S], BF16)
        maxima = sb("maxima", [P, 2, 4, KT])
        mrest = sb("mrest", [4 * KT, P])
        mparts = sb("mparts", [4 * KT, 2, 3, P], BF16)
        xrows = sb("xrows", [P, 2, 2, D])
        slots = sb("slots", [P, 2, 2, 2], I32)
        mpsum = ctx.enter_context(nc.psum_tensor("mpsum", [P, 2, S], F32))
        spsum = ctx.enter_context(nc.psum_tensor("spsum", [P, 2, CH], F32))
        cpsum = ctx.enter_context(nc.psum_tensor("cpsum", [P, 2, CH], F32))

        stack_in = [sem(f"stack_in{i}") for i in range(NQ)]
        const_in = sem("const_in")
        v_in = [sem(f"v_in{i}") for i in range(NQ)]
        mrow_in = [sem(f"mrow_in{i}") for i in range(NQ)]
        cleared = sem("cleared")
        passed = sem("passed3")
        m_ready = sem("m_ready")
        m_taken = sem("m_taken")
        max_step = sem("max_step")
        max_split = sem("max_split")
        s_ready = sem("s_ready")
        exp_done = sem("exp_done")
        masked = sem("masked")
        pv_done = sem("pv_done")
        ctx_taken = sem("ctx_taken")
        rows_in = [sem(f"rows_in{i}") for i in range(2)]
        rows_out = [sem(f"rows_out{i}") for i in range(2)]
        block = ctx.enter_context(nc.Block())
        RING = 2

        def wait_apart(eng, sem, value):
            eng.wait_ge(sem, value)
            eng.sem_inc(passed, 1)

        STACK_DMAS = 2 * len(Q_PART)

        def steps(eng, body):
            with eng.Fori(0, B - 1) as b:
                for hq in range(NQ):
                    body(NQ * b + hq, b, hq, lambda j: True)
            for hq in range(NQ):
                body(NQ * (B - 1) + hq, B - 1, hq, lambda j, hq=hq: hq + j < NQ)

        def quad(b, hq, j):
            return b + (hq + j) // NQ, (hq + j) % NQ

        @block.sync
        def _(sp):
            for q in range(NQ):
                sp.dma_start(qs[q][R_ALIBI:R_MAX, :, :], ins["c_q"][q]).then_inc(const_in, 16)
                sp.dma_start(ks[q][R_ALIBI:ROWS, :, :], ins["c_k"]).then_inc(const_in, 16)

            def load(b, hq):
                parts_of = scratch["qk"][hq]
                for r in range(len(Q_PART)):
                    for side, dst, part in ((0, qs[hq], Q_PART[r]), (1, ks[hq], K_PART[r])):
                        src = parts_of[part, 4 * HD * side:4 * HD * (side + 1), ds(S * b, S)]
                        sp.dma_start(dst[HD * r:HD * (r + 1), :, :], src.rearrange("(h d) t -> d h t", d=HD)).then_inc(stack_in[hq], 16)
                sp.dma_start(vs[hq][:, :, :, :].rearrange("p t h w -> p t (h w)"),
                             scratch["v"][hq][ds(S * b, S), :].rearrange("(t p) w -> p t w", p=P)).then_inc(v_in[hq], 16)

            def maxima_rows(n, hq):
                sp.wait_ge(max_split, n + 1)
                for j in range(3):
                    sp.dma_start(qs[hq][R_MAX + j:R_MAX + j + 1, :, :], mparts[:, hq % 2, j, :]).then_inc(mrow_in[hq], 16)

            def tile_rows(t, par):
                sp.dma_start(xrows[:, par], scratch["xn"].rearrange("(i p) d -> p i d", p=P)[:, ds(2 * t, 2), :]).then_inc(rows_in[par], 16)
                sp.dma_start(slots[:, par], keep["slot"][:, :, ds(2 * t, 2)]).then_inc(rows_in[par], 16)

            for hq in range(3):
                load(0, hq)
            for t in range(2):
                tile_rows(t, t)
            maxima_rows(0, 0)

            def body(t, b, hq, has):
                par = hq % 2
                if has(3):
                    sp.wait_ge(pv_done, PRING + NU * t)
                    load(*quad(b, hq, 3))
                if has(1):
                    maxima_rows(t + 1, (hq + 1) % NQ)
                sp.wait_ge(rows_out[par], 64 * (2 * b + hq // 2 + 1))
                if has(2):
                    tile_rows(t + 2, par)

            steps(sp, body)
            for i in range(2):
                sp.wait_ge(rows_out[i], 64 * (B * NQ // 2))

        @block.gpsimd
        def _(pool):
            def body(t, b, hq, has):
                par = hq % 2
                wait_apart(pool, rows_in[par], 32 * (2 * b + hq // 2 + 1))
                for i in range(2):
                    for k in range(2):
                        pool.indirect_dma_start(scratch["xs"], bass.IndirectOffsetOnAxis(ap=slots[:, par, k, i:i + 1].bitcast(U32), axis=0),
                                                xrows[:, par, i, :], None).then_inc(rows_out[par], 16)
                for j in range(1, NU + 1):
                    if j == NU and not has(1):
                        continue
                    mask_unit(NU * t + j, j % NU)

            def mask_unit(n, u):
                if not DIAG[u]:
                    return
                wait_apart(pool, exp_done, 4 * n + 4 + RING)
                for c in DIAG[u]:
                    part = probs[:, u % PRING, :, c:c + P]
                    pool.affine_select(out=part, in_=part, compare_op=ALU.is_ge, fill=0.0, base=0,
                                       pattern=[[0, 4], [1, P]], channel_multiplier=-1).then_inc(masked, 1)

            mask_unit(0, 0)
            steps(pool, body)

        @block.vector
        def _(dve):
            dve.sem_inc(m_taken, RING)
            dve.memset(cpsum[:, :, :], 0.0).then_inc(cleared, 1)

            def item(t, hq, k):
                n = NI * t + k
                slot = (NI * hq + k) % RING
                dve.wait_ge(m_taken, n + 1)
                wait_apart(dve, m_ready, n + 1)
                if k < NI - 1:
                    h, qt = ITEMS[k]
                    w = (qt + 1) * P
                    last = dve.tensor_tensor_reduce(junk[:, slot, 0:w], mpsum[:, slot, 0:w], keep["mask"][:, S - w:S], 1.0, 3 * NEG,
                                                    ALU.add, ALU.max, maxima[:, hq % 2, h, qt:qt + 1])
                    last.then_inc(m_taken, 1)
                    return
                mT = mpsum[0:4 * KT, slot, 0:P]
                parts = mparts[:, hq % 2]
                dve.tensor_scalar(parts[:, 0], mT, -1.0, None, ALU.mult).then_inc(max_step, 1)
                dve.wait_ge(max_step, 3 * t + 1)
                dve.scalar_tensor_tensor(mrest[:, :], mT, -1.0, parts[:, 0], ALU.mult, ALU.subtract).then_inc(m_taken, 1)
                dve.wait_ge(m_taken, n + 1 + RING)
                dve.tensor_copy(parts[:, 1], mrest[:, :]).then_inc(max_step, 1)
                dve.wait_ge(max_step, 3 * t + 2)
                dve.tensor_tensor(parts[:, 2], mrest[:, :], parts[:, 1], ALU.subtract).then_inc(max_step, 1)
                dve.wait_ge(max_step, 3 * t + 3)
                dve.sem_inc(max_split, 1)

            for k in range(NI):
                item(0, 0, k)
            for k in range(LEAD):
                item(1, 1, k)

            def body(t, b, hq, has):
                for slot in SLOT_ITEMS:
                    for j, k in slot:
                        if has(j):
                            item(t + j, (hq + j) % NQ, k)

            steps(dve, body)

        @block.scalar
        def _(act):
            act.sem_inc(exp_done, RING)

            def exps(n, u, heads):
                for h in heads:
                    m = 4 * n + h
                    act.wait_ge(s_ready, m + 1)
                    if h == 0:
                        act.wait_ge(pv_done, n + 1)
                    act.activation(probs[:, u % PRING, h], spsum[:, h % 2], ACT.Exp, scale=SCALE).then_inc(exp_done, 1)

            exps(0, 0, range(4))

            def body(t, b, hq, has):
                for u in range(1, NU):
                    exps(NU * t + u, u, range(4))
                if has(1):
                    exps(NU * t + NU, 0, range(4))
                act.wait_ge(pv_done, NU * t + NU + PRING)
                act.activation(keep["ctxT"][:, ds(t, 1), 0:CH].rearrange("p a c -> p (a c)"), cpsum[:, 0], ACT.Copy)
                act.activation(keep["ctxT"][:, ds(t, 1), CH:S].rearrange("p a c -> p (a c)"), cpsum[:, 1], ACT.Copy).then_inc(ctx_taken, 1)

            steps(act, body)

        @block.tensor
        def _(pe):
            pe.sem_inc(pv_done, PRING)
            pe.sem_inc(ctx_taken, 1)
            pe.wait_ge(cleared, 1)
            pe.wait_ge(const_in, 16 * 2 * NQ)

            def item(t, b, hq, k):
                n = NI * t + k
                slot = (NI * hq + k) % RING
                if k == 0:
                    pe.wait_ge(stack_in[hq], 16 * STACK_DMAS * (b + 1))
                pe.wait_ge(m_taken, n + 1)
                if k < NI - 1:
                    h, qt = ITEMS[k]
                    w = (qt + 1) * P
                    for c in range(0, w, CH):
                        e = min(w, c + CH)
                        last = pe.matmul(mpsum[:, slot, c:e], qs[hq][0:R_MAX, h, qt * P:(qt + 1) * P], ks[hq][0:R_MAX, h, c:e],
                                         start=True, stop=True)
                    last.then_inc(m_ready, 1)
                else:
                    pe.wait_ge(m_taken, n + RING)
                    pe.transpose(mpsum[0:4 * KT, slot, 0:P], maxima[:, hq % 2].rearrange("p h q -> p (h q)"), keep["ident"][:, :]).then_inc(m_ready, 1)

            def scores(n, hq, u, h):
                m = 4 * n + h
                pe.wait_ge(exp_done, m + 1)
                for c, kt, q0, w in UNITS[u]:
                    last = pe.matmul(spsum[:, h % 2, c:c + w], ks[hq][:, h, kt * P:(kt + 1) * P], qs[hq][:, h, q0:q0 + w],
                                     start=True, stop=True)
                last.then_inc(s_ready, 1)

            def weighted(n, t, b, hq, u):
                pe.wait_ge(exp_done, 4 * n + 4 + RING)
                if DIAG[u]:
                    pe.wait_ge(masked, MASKED[NU] * t + MASKED[u + 1])
                if u == 0:
                    pe.wait_ge(v_in[hq], 16 * (b + 1))
                    pe.wait_ge(ctx_taken, t + 1)
                for c, kt, q0, w in UNITS[u]:
                    half = q0 // CH
                    for h in range(4):
                        last = pe.matmul(cpsum[32 * h:32 * h + VW, half, q0 - half * CH:q0 - half * CH + w], vs[hq][:, kt, h], probs[:, u % PRING, h, c:c + w],
                                         start=kt == 0, stop=kt == (3 if half == 0 else 7), tile_position=(0, 32 * h), skip_group_check=True)
                last.then_inc(pv_done, 1)

            for k in range(NI):
                item(0, 0, 0, k)
            pe.wait_ge(mrow_in[0], 48)
            for k in range(LEAD):
                item(1, 0, 1, k)
                if k % 3 == 0:
                    scores(0, 0, 0, k // 3)

            def body(t, b, hq, has):
                for j in range(1, NU + 1):
                    u, n = j % NU, NU * t + j
                    b1, hq1 = quad(b, hq, 1) if j == NU else (b, hq)
                    for h in range(4):
                        if j < NU or has(1):
                            if u == 0 and h == 0:
                                pe.wait_ge(mrow_in[hq1], 48 * (b1 + 1))
                            scores(n, hq1, u, h)
                        for ahead, k in SLOT_ITEMS[4 * (j - 1) + h]:
                            if has(ahead):
                                item(t + ahead, *quad(b, hq, ahead), k)
                    weighted(n - 1, t, b, hq, j - 1)

            steps(pe, body)


def experts(nc, ins, scratch, keep):
    with ExitStack() as ctx:
        sb = lambda name, shape, dt=F32: ctx.enter_context(nc.sbuf_tensor(name, shape, dt))
        sem = lambda name: ctx.enter_context(nc.semaphore(name))
        w_gu = sb("w_gu", [P, NE * DH, 2 * HID])
        w_down = sb("w_down", [P, NE * DH, D])
        rows = sb("rows", [P, 2, D])
        xT = sb("xTs", [P, 2, DH, P])
        gate = sb("gate", [P, 2, HID])
        hid = sb("hid", [P, 2, HID])
        hT = sb("hT", [P, 2, DH, P])
        y = sb("y", [P, 2, D])
        tp = ctx.enter_context(nc.psum_tensor("tp", [P, 2, CH], F32))
        gu = ctx.enter_context(nc.psum_tensor("gu", [P, 2, CH], F32))
        hp = ctx.enter_context(nc.psum_tensor("hp", [P, 2, CH], F32))
        yp = ctx.enter_context(nc.psum_tensor("yp", [P, 2, CH], F32))
        w_in = sem("w_in")
        rows_in = [sem(f"srows_in{i}") for i in range(2)]
        y_out = [sem(f"y_out{i}") for i in range(2)]
        tp_ready, xT_ready = sem("tps_ready"), sem("xTs_ready")
        gu_ready, gate_ready, hid_ready = sem("gu_ready"), sem("gate_ready"), sem("hid_ready")
        hp_ready, hT_ready = sem("hp_ready"), sem("hT_ready")
        yp_ready, y_ready = sem("yp_ready"), sem("y_ready")
        block = ctx.enter_context(nc.Block())
        xs = scratch["xs"].rearrange("(s p) d -> s p d", p=P)
        ys = scratch["ys"].rearrange("(s p) d -> s p d", p=P)

        def tiles(eng, body):
            with eng.Fori(0, NST // 2) as i:
                for par in range(2):
                    body(2 * i + par, par, i)

        @block.sync
        def _(sp):
            for e in range(NE):
                sp.dma_start(w_gu[:, e * DH:(e + 1) * DH], ins["w_gu"][:, e * DH:(e + 1) * DH]).then_inc(w_in, 16)
                sp.dma_start(w_down[:, e * DH:(e + 1) * DH], ins["w_down"][:, e * DH:(e + 1) * DH]).then_inc(w_in, 16)
                if e == 0:
                    sp.sem_inc(tp_ready, 2)

            def body(s, par, i):
                sp.wait_ge(tp_ready, s + 1)
                sp.dma_start(rows[:, par], xs[ds(s, 1)].rearrange("a p d -> (a p) d")).then_inc(rows_in[par], 16)

            tiles(sp, body)

        @block.scalar
        def _(act):
            for i in range(2):
                act.sem_inc(y_out[i], 16)

            def xT_copy(s, par):
                act.wait_ge(tp_ready, s + 1 + 2)
                act.activation(xT[:, par].rearrange("p a t -> p (a t)"), tp[:, par, 0:D], ACT.Copy).then_inc(xT_ready, 1)

            def gelu(s, par):
                act.wait_ge(gu_ready, s + 1)
                act.activation(gate[:, par], gu[:, par, 0:HID], ACT.Gelu_apprx_tanh).then_inc(gate_ready, 1)

            def store(s, par, i):
                act.wait_ge(yp_ready, s + 1)
                act.wait_ge(y_out[par], 16 * (i + 1))
                act.activation(y[:, par], yp[:, par, 0:D], ACT.Copy).then_inc(y_ready, 1)
                act.wait_ge(y_ready, s + 1)
                act.dma_start(ys[ds(s, 1)].rearrange("a p d -> (a p) d"), y[:, par]).then_inc(y_out[par], 16)

            xT_copy(0, 0)
            gelu(0, 0)
            xT_copy(1, 1)
            gelu(1, 1)
            xT_copy(2, 0)
            with act.Fori(0, NST // 2 - 2) as i:
                for par in range(2):
                    s = 2 * i + 2 + par
                    gelu(s, par)
                    xT_copy(s + 1, 1 - par)
                    store(s - 2, par, i)
            gelu(NST - 2, 0)
            xT_copy(NST - 1, 1)
            store(NST - 4, 0, NST // 2 - 2)
            gelu(NST - 1, 1)
            for s in range(NST - 3, NST):
                store(s, s % 2, s // 2)
            for i in range(2):
                act.wait_ge(y_out[i], 16 + 16 * (NST // 2))

        @block.vector
        def _(dve):
            def body(s, par, i):
                dve.wait_ge(gate_ready, s + 1)
                dve.tensor_tensor(hid[:, par], gu[:, par, HID:2 * HID], gate[:, par], ALU.mult).then_inc(hid_ready, 1)
                dve.wait_ge(hp_ready, s + 1)
                dve.tensor_copy(hT[:, par].rearrange("p a t -> p (a t)"), hp[:, par, 0:HID]).then_inc(hT_ready, 1)

            tiles(dve, body)

        @block.tensor
        def _(pe):
            pe.wait_ge(w_in, 16 * 2 * NE)

            def rows_T(s, par, i):
                pe.wait_ge(rows_in[par], 16 * (i + 1))
                for dh in range(DH):
                    last = pe.transpose(tp[:, par, dh * P:(dh + 1) * P], rows[:, par, dh * P:(dh + 1) * P], keep["ident"][:, :])
                last.then_inc(tp_ready, 1)

            def gate_up(s, par):
                e = pe.value_load(keep["tile_expert"][0:1, ds(s, 1)], min_val=0, max_val=NE - 1)
                pe.wait_ge(xT_ready, s + 1)
                for dh in range(DH):
                    last = pe.matmul(gu[:, par], xT[:, par, dh], w_gu[:, ds(e * DH + dh, 1)].rearrange("p a c -> p (a c)"),
                                     start=dh == 0, stop=dh == DH - 1)
                last.then_inc(gu_ready, 1)

            def hidden_T(s, par):
                pe.wait_ge(hid_ready, s + 1)
                for dh in range(DH):
                    last = pe.transpose(hp[:, par, dh * P:(dh + 1) * P], hid[:, par, dh * P:(dh + 1) * P], keep["ident"][:, :])
                last.then_inc(hp_ready, 1)

            def down(s, par):
                e = pe.value_load(keep["tile_expert"][0:1, ds(s, 1)], min_val=0, max_val=NE - 1)
                pe.wait_ge(hT_ready, s + 1)
                for dh in range(DH):
                    last = pe.matmul(yp[:, par, 0:D], hT[:, par, dh], w_down[:, ds(e * DH + dh, 1)].rearrange("p a c -> p (a c)"),
                                     start=dh == 0, stop=dh == DH - 1)
                last.then_inc(yp_ready, 1)

            rows_T(0, 0, 0)
            gate_up(0, 0)
            rows_T(1, 1, 0)
            gate_up(1, 1)
            hidden_T(0, 0)
            rows_T(2, 0, 1)
            with pe.Fori(0, NST // 2 - 2) as i:
                for par in range(2):
                    s = 2 * i + 2 + par
                    gate_up(s, par)
                    hidden_T(s - 1, 1 - par)
                    rows_T(s + 1, 1 - par, i + 1 + par)
                    down(s - 2, par)
            gate_up(NST - 2, 0)
            hidden_T(NST - 3, 1)
            rows_T(NST - 1, 1, NST // 2 - 1)
            down(NST - 4, 0)
            gate_up(NST - 1, 1)
            hidden_T(NST - 2, 0)
            down(NST - 3, 1)
            hidden_T(NST - 1, 1)
            down(NST - 2, 0)
            pe.wait_ge(y_ready, NST - 2)
            down(NST - 1, 1)


def combine(nc, ins, scratch, keep, out):
    with ExitStack() as ctx:
        sb = lambda name, shape, dt=F32: ctx.enter_context(nc.sbuf_tensor(name, shape, dt))
        sem = lambda name: ctx.enter_context(nc.semaphore(name))
        NP, PB = NT // 2, KT // 2
        LOADS = 4
        w_o = sb("w_o", [P, DH, D])
        bias = sb("bias", [P, D])
        sums = sb("sums", [P, PB, NQ, 2 * P])
        xr = sb("xr", [P, PB, 2, D])
        slots = sb("slots_c", [P, PB, 2, 2], I32)
        wts = sb("wts", [P, PB, 2, 2])
        inv = sb("inv", [P, 2, NH])
        ctxn = sb("ctxn", [P, 2, NH, HD])
        ctxnT = sb("ctxnT", [P, 2, 2, D])
        yk = sb("yk", [P, 2, 2, 2, D])
        xb = sb("xb", [P, 2, D])
        acc = sb("acc", [P, 3, 2, D])
        done = sb("done", [P, 2, 2, D])
        sumsT = ctx.enter_context(nc.psum_tensor("sumsT", [P, 2, CH], F32))
        backT = ctx.enter_context(nc.psum_tensor("backT", [P, 2, CH], F32))
        proj = ctx.enter_context(nc.psum_tensor("proj", [P, 2, CH], F32))
        w_in = sem("wo_in")
        passed = sem("passed5")
        loaded = [sem(f"loaded{i}") for i in range(PB)]
        y_in = [sem(f"y_in{i}") for i in range(2)]
        out_done = [sem(f"out_done{i}") for i in range(2)]
        sumsT_ready, inv_ready, norm_ready = sem("sumsT_ready"), sem("inv_ready"), sem("norm_ready")
        backT_ready, ctxnT_ready, proj_ready = sem("backT_ready"), sem("ctxnT_ready"), sem("proj_ready")
        xb_ready, acc_ready, one_ready, pair_done = sem("xb_ready"), sem("acc_ready"), sem("one_ready"), sem("pair_done")
        block = ctx.enter_context(nc.Block())
        x_rows = ins["x"].rearrange("(g p) d -> p g d", p=P)
        out_rows = out.rearrange("(g p) d -> p g d", p=P)
        RING = 2

        def pairs(eng, body):
            with eng.Fori(0, B - 1) as b:
                for p in range(1, PB + 1):
                    body(b, p)
            for p in range(1, PB + 1):
                body(B - 1, p)

        def exists(b, p):
            return not isinstance(b, int) or PB * b + p < NP

        @block.sync
        def _(sp):
            sp.dma_start(w_o[:, :, :], ins["w_o"]).then_inc(w_in, 16)
            sp.dma_start(bias[:, :], ins["bo"].partition_broadcast(P)).then_inc(w_in, 16)
            for i in range(2):
                sp.sem_inc(out_done[i], 16)

            def load(b, p):
                g = 2 * (PB * b + p)
                sp.dma_start(sums[:, p], keep["ctxT"][:, ds(NQ * b, NQ), 2 * P * p:2 * P * (p + 1)]).then_inc(loaded[p], 16)
                sp.dma_start(xr[:, p], x_rows[:, ds(g, 2), :]).then_inc(loaded[p], 16)
                sp.dma_start(slots[:, p], keep["slot"][:, :, ds(g, 2)]).then_inc(loaded[p], 16)
                sp.dma_start(wts[:, p], keep["weight"][:, :, ds(g, 2)]).then_inc(loaded[p], 16)

            def store(b, p):
                sp.wait_ge(pair_done, PB * b + p + 1 + RING)
                sp.dma_start(out_rows[:, ds(2 * (PB * b + p), 2), :], done[:, p % 2]).then_inc(out_done[p % 2], 16)

            for p in range(PB):
                load(0, p)
            with sp.Fori(0, B - 1) as b:
                for p in range(PB):
                    store(b, p)
                    load(b + 1, p)
            for p in range(PB):
                store(B - 1, p)
            for i in range(2):
                sp.wait_ge(out_done[i], 16 + 16 * (NP // 2))

        @block.gpsimd
        def _(pool):
            with pool.Fori(0, B) as b:
                for p in range(PB):
                    pool.wait_ge(loaded[p], 16 * LOADS * (b + 1))
                    pool.wait_ge(pair_done, PB * b + p + 1)
                    pool.sem_inc(passed, 1)
                    for t in range(2):
                        for k in range(2):
                            pool.indirect_dma_start(yk[:, p % 2, t, k], None, scratch["ys"],
                                                    bass.IndirectOffsetOnAxis(ap=slots[:, p, k, t:t + 1].bitcast(U32), axis=0)).then_inc(y_in[p % 2], 16)

        @block.tensor
        def _(pe):
            pe.sem_inc(norm_ready, 1)
            pe.wait_ge(w_in, 32)

            def turn(b, p):
                p, b = p % PB, b + p // PB
                pe.wait_ge(loaded[p], 16 * LOADS * (b + 1))
                pe.wait_ge(norm_ready, PB * b + p + 1)
                for t in range(2):
                    for q in range(NQ):
                        last = pe.transpose(sumsT[:, t, P * q:P * (q + 1)], sums[:, p, q, P * t:P * (t + 1)], keep["ident"][:, :])
                last.then_inc(sumsT_ready, 1)

            def turn_back(b, p):
                p, b = p % PB, b + p // PB
                pe.wait_ge(norm_ready, PB * b + p + 2)
                for t in range(2):
                    for dh in range(DH):
                        last = pe.transpose(backT[:, p % 2, D * t + P * dh:D * t + P * (dh + 1)],
                                            ctxn[:, t].rearrange("p h w -> p (h w)")[:, P * dh:P * (dh + 1)], keep["ident"][:, :])
                last.then_inc(backT_ready, 1)

            def project_pair(b, p):
                p, b = p % PB, b + p // PB
                pe.wait_ge(ctxnT_ready, PB * b + p + 1)
                for t in range(2):
                    for dh in range(DH):
                        last = pe.matmul(proj[:, p % 2, D * t:D * (t + 1)], ctxnT[:, p % 2, t, P * dh:P * (dh + 1)], w_o[:, dh],
                                         start=dh == 0, stop=dh == DH - 1)
                last.then_inc(proj_ready, 1)

            turn(0, 0)
            turn_back(0, 0)
            turn(0, 1)

            def body(b, p):
                if exists(b, p):
                    turn_back(b, p)
                    if exists(b, p + 1):
                        turn(b, p + 1)
                project_pair(b, p - 1)

            pairs(pe, body)

        @block.scalar
        def _(act):
            with act.Fori(0, B) as b:
                for p in range(PB):
                    act.wait_ge(backT_ready, PB * b + p + 1)
                    act.wait_ge(pair_done, PB * b + p + 1)
                    act.activation(ctxnT[:, p % 2].rearrange("p t c -> p (t c)"), backT[:, p % 2], ACT.Copy).then_inc(ctxnT_ready, 1)

        @block.vector
        def _(dve):
            dve.sem_inc(pair_done, RING)
            dve.wait_ge(w_in, 32)

            def normalise(b, p):
                p, b = p % PB, b + p // PB
                n = PB * b + p
                dve.wait_ge(sumsT_ready, n + 1)
                heads = sumsT[:, :, :].rearrange("p t (h w) -> p t h w", w=32)
                for t in range(2):
                    dve.reciprocal(inv[:, t], heads[:, t, :, HD]).then_inc(inv_ready, 1)
                if not isinstance(b, int) or n > 0:
                    dve.wait_ge(backT_ready, n)
                dve.wait_ge(inv_ready, 2 * n + 2)
                for t in range(2):
                    last = dve.tensor_tensor(ctxn[:, t], heads[:, t, :, 0:HD],
                                             inv[:, t].rearrange("p (h a) -> p h a", a=1).to_broadcast([P, NH, HD]), ALU.mult)
                last.then_inc(norm_ready, 1)

            def add_input(b, p):
                p, b = p % PB, b + p // PB
                dve.wait_ge(loaded[p], 16 * LOADS * (b + 1))
                dve.tensor_tensor(xb[:, :, :], xr[:, p], bias[:, :].rearrange("p (a d) -> p a d", a=1).to_broadcast([P, 2, D]), ALU.add).then_inc(xb_ready, 1)

            def total_up(b, p):
                p, b = p % PB, b + p // PB
                n = PB * b + p
                dve.wait_ge(proj_ready, n + 1)
                dve.wait_ge(xb_ready, n + 1)
                dve.tensor_tensor(acc[:, 0].rearrange("p t d -> p (t d)"), proj[:, p % 2], xb[:, :, :].rearrange("p t d -> p (t d)"), ALU.add).then_inc(acc_ready, 1)
                dve.wait_ge(acc_ready, n + 1)
                dve.wait_ge(y_in[p % 2], 64 * (PB // 2 * b + p // 2 + 1))
                for t in range(2):
                    dve.scalar_tensor_tensor(acc[:, 1, t], yk[:, p % 2, t, 0], wts[:, p, 0, t:t + 1], acc[:, 0, t], ALU.mult, ALU.add).then_inc(one_ready, 1)
                dve.wait_ge(out_done[p % 2], 16 * (PB // 2 * b + p // 2 + 1))
                for t in range(2):
                    dve.wait_ge(one_ready, 2 * n + t + 1)
                    last = dve.scalar_tensor_tensor(done[:, p % 2, t], yk[:, p % 2, t, 1], wts[:, p, 1, t:t + 1], acc[:, 1, t], ALU.mult, ALU.add)
                last.then_inc(pair_done, 1)

            normalise(0, 0)
            normalise(0, 1)

            def body(b, p):
                if exists(b, p + 1):
                    normalise(b, p + 1)
                add_input(b, p - 1)
                total_up(b, p - 1)

            pairs(dve, body)


def build(nc, ins, out):
    with ExitStack() as ctx:
        sb = lambda name, shape, dt=F32: ctx.enter_context(nc.sbuf_tensor(name, shape, dt))
        keep = {
            "ident": sb("ident", [P, P]),
            "mhalf": sb("mhalf", [P, NT]),
            "mask": sb("mask", [P, S]),
            "msq": sb("msq", [P, NT]),
            "logits": sb("logits", [P, NT, NE]),
            "weight": sb("weight", [P, 2, NT]),
            "slot": sb("slot", [P, 2, NT], I32),
            "tile_expert": sb("tile_expert", [1, NST], I32),
            "ctxT": sb("ctxT", [P, B * NQ, S]),
        }
        scratch = {
            "xn": nc.dram_tensor("xn_rows", [TOK, D], F32).ap(),
            "qk": nc.dram_tensor("qk_parts", [NQ, 3, P, TOK], BF16).ap(),
            "v": nc.dram_tensor("v_rows", [NQ, TOK, 4 * VW], F32).ap(),
            "xs": nc.dram_tensor("slot_rows", [NST * P, D], F32).ap(),
            "ys": nc.dram_tensor("expert_rows", [NST * P, D], F32).ap(),
        }
        project(nc, ins, scratch, keep)
        route(nc, ins, scratch, keep)
        attend(nc, ins, scratch, keep)
        experts(nc, ins, scratch, keep)
        combine(nc, ins, scratch, keep, out)


def bf16_bits(a):
    bits = np.asarray(a, np.float32).view(np.uint32)
    return (bits >> 16).astype(np.uint16)


def constants():
    slopes = (2.0 ** (-8.0 * np.arange(1, NH + 1) / NH)).astype(np.float32)
    parts, rest = [], slopes.copy()
    for _ in range(3):
        top = (rest.view(np.uint32) & np.uint32(0xFFFF0000)).view(np.float32)
        parts.append(top)
        rest = rest - top
    c_q = np.zeros((NQ, 6, 4, S), np.float32)
    for j in range(6):
        c_q[:, j] = parts[j % 3].reshape(NQ, 4, 1)
    pos = np.arange(S)
    c_k = np.ones((9, 4, S), np.float32)
    c_k[0:3] = (pos // 256 * 256)[None, None, :]
    c_k[3:6] = (pos % 256)[None, None, :]
    return bf16_bits(c_q), bf16_bits(c_k)


def kernel(L0_attn_x, L0_attn_Wq, L0_attn_Wk, L0_attn_Wv, L0_attn_Wo, L0_attn_bo, L0_ffn_router_logits,
           L0_ffn_gating_einsum, L0_ffn_linear, L0_ffn_per_expert_scale, L0_ffn_router_scale):
    import concourse.bacc as bacc
    from concourse.bass_utils import run_bass_kernel_spmd

    split = lambda w: np.asarray(w).reshape(DH, P, -1).transpose(1, 0, 2)
    wq, wk = (split(w).reshape(P, DH, NQ, 4 * HD) for w in (L0_attn_Wq, L0_attn_Wk))
    w_gu = np.asarray(L0_ffn_gating_einsum).reshape(NE, 2 * HID, DH, P).transpose(3, 0, 2, 1)
    w_down = np.asarray(L0_ffn_linear).reshape(NE, DH, P, D).transpose(2, 0, 1, 3)
    c_q, c_k = constants()
    arrays = {
        "x": np.asarray(L0_attn_x).reshape(TOK, D),
        "w_qk": np.concatenate([wq, wk], axis=3),
        "w_v": split(L0_attn_Wv),
        "w_r": split(L0_ffn_router_logits),
        "router_scale": np.asarray(L0_ffn_router_scale).reshape(DH, P).T,
        "w_o": split(L0_attn_Wo),
        "bo": np.asarray(L0_attn_bo),
        "w_gu": w_gu.reshape(P, NE * DH, 2 * HID),
        "w_down": w_down.reshape(P, NE * DH, D),
        "expert_scale": np.asarray(L0_ffn_per_expert_scale),
        "c_q": c_q,
        "c_k": c_k,
    }
    arrays = {"in_" + k: np.ascontiguousarray(v) for k, v in arrays.items()}
    nc = bacc.Bacc("TRN2", target_bir_lowering=False, num_devices=1)
    ins = {}
    for name, a in arrays.items():
        ap = nc.dram_tensor(name, a.shape, mybir.dt.from_np(a.dtype), kind="ExternalInput").ap()
        ins[name[3:]] = ap.bitcast(BF16) if a.dtype == np.uint16 else ap
    out = nc.dram_tensor("out", (TOK, D), F32, kind="ExternalOutput").ap()
    build(nc, ins, out)
    r = run_bass_kernel_spmd(nc, [arrays], core_ids=[0])
    return r.results[0]["out"].reshape(B, S, D)
```

```python
from contextlib import ExitStack

import concourse.bass as bass
from concourse import mybir
import numpy as np

P = 128
F32 = mybir.dt.float32
BF16 = mybir.dt.bfloat16
I32 = mybir.dt.int32
U32 = mybir.dt.uint32
U16 = mybir.dt.uint16
ALU = mybir.AluOpType
ACT = mybir.ActivationFunctionType
AX_X = mybir.AxisListType.X
ds = bass.ds

B, S, D = 4, 1024, 256
NH, HD = 16, 16
TOK = B * S
NT = TOK // P
DH = D // P
NQ = NH // 4
NE, HID = 8, 256
CH = 512
NC = TOK // CH
NST = 2 * TOK // P + NE
LN_EPS, RMS_EPS = 1e-5, 1e-6
NEG = -1e30
KT = S // P

Q_PART = [0, 1, 2, 0, 1, 0]
K_PART = [0, 0, 0, 1, 1, 2]
R_ALIBI = 6 * HD
R_MAX = R_ALIBI + 6
ROWS = R_MAX + 3
VW = HD + 1
SCALE = float(HD) ** -0.5

UNITS = [
    [(0, 0, 0, 512)],
    [(0, 0, 512, 512)],
    [(0, 1, 128, 384), (384, 3, 384, 128)],
    [(0, 1, 512, 512)],
    [(0, 2, 256, 256), (256, 6, 768, 256)],
    [(0, 2, 512, 512)],
    [(0, 3, 512, 512)],
    [(0, 4, 512, 512)],
    [(0, 5, 640, 384), (384, 7, 896, 128)],
]
NU = len(UNITS)
DIAG = [[c for c, kt, q0, _ in u if q0 == kt * P] for u in UNITS]
MASKED = [sum(map(len, DIAG[:u])) for u in range(NU + 1)]


def pv_halves(unit):
    diagonal = [(c, kt, q0, P) for c, kt, q0, _ in unit if q0 == kt * P]
    if diagonal:
        return [(c + P, kt, q0 + P, w - P) for c, kt, q0, w in unit if w > P], diagonal
    (c, kt, q0, w), = unit
    return [(c, kt, q0, w // 2)], [(c + w // 2, kt, q0 + w // 2, w // 2)]


PV = [pv_halves(u) for u in UNITS]
PRING = 3

ITEMS = [(h, qt) for h in range(4) for qt in (7, 0, 1, 6, 5, 2, 3, 4)]
NI = len(ITEMS) + 1
LEAD = 12
SLOTS = 4 * NU
FIRST_PART = 24


def slot_items():
    ahead1 = [(1, k) for k in range(LEAD, NI)]
    ahead2 = [(2, k) for k in range(LEAD)]
    out, done = [], 0
    for s in range(SLOTS):
        if s < FIRST_PART:
            upto = (s + 1) * len(ahead1) // FIRST_PART
            out.append(ahead1[done:upto])
            done = upto
        else:
            n = s - FIRST_PART
            out.append(ahead2[n:n + 1])
    return out


SLOT_ITEMS = slot_items()
assert sum(map(len, SLOT_ITEMS)) == NI


def head_buffers(nc, ctx):
    sb = lambda name, shape, dt=F32: ctx.enter_context(nc.sbuf_tensor(name, shape, dt))
    sem = lambda name: ctx.enter_context(nc.semaphore(name))
    return {
        "qs": [sb(f"qs{i}", [ROWS, 4, S], BF16) for i in range(NQ)],
        "ks": [sb(f"ks{i}", [ROWS, 4, S], BF16) for i in range(NQ)],
        "vs": [sb(f"vs{i}", [P, KT, 4, VW]) for i in range(NQ)],
        "stack_in": [sem(f"stack_in{i}") for i in range(NQ)],
        "v_in": [sem(f"v_in{i}") for i in range(NQ)],
        "const_in": sem("const_in"),
    }


STACK_DMAS = 2 * len(Q_PART)


def load_quad(sp, scratch, heads, b, hq):
    parts_of = scratch["qk"][hq]
    for r in range(len(Q_PART)):
        for side, dst, part in ((0, heads["qs"][hq], Q_PART[r]), (1, heads["ks"][hq], K_PART[r])):
            src = parts_of[part, 4 * HD * side:4 * HD * (side + 1), ds(S * b, S)]
            sp.dma_start(dst[HD * r:HD * (r + 1), :, :], src.rearrange("(h d) t -> d h t", d=HD)).then_inc(heads["stack_in"][hq], 16)
    sp.dma_start(heads["vs"][hq][:, :, :, :].rearrange("p t h w -> p t (h w)"),
                 scratch["v"][hq][ds(S * b, S), :].rearrange("(t p) w -> p t w", p=P)).then_inc(heads["v_in"][hq], 16)


def project(nc, ins, scratch, keep):
    with ExitStack() as ctx:
        sb = lambda name, shape, dt=F32: ctx.enter_context(nc.sbuf_tensor(name, shape, dt))
        ps = lambda name, shape: ctx.enter_context(nc.psum_tensor(name, shape, F32))
        sem = lambda name: ctx.enter_context(nc.semaphore(name))
        w_qk = sb("w_qk", [P, DH, NQ, P])
        w_vr = sb("w_vr", [P, DH, D + NE])
        rscale = sb("rscale", [P, DH])
        ident, mhalf = keep["ident"], keep["mhalf"]
        x_in = sb("x_in", [P, 2, 4, D])
        xn = sb("xn", [P, 2, 4, D])
        stats = sb("stats", [P, 2, 4, 6])
        mv = sb("mv", [P, 2, 4, 2])
        veps = sb("veps", [P, 2, 4])
        rstd = sb("rstd", [P, 2, 4])
        rsq = sb("rsq", [P, 2, 4])
        xT = sb("xT", [P, 2, DH, CH])
        rest = sb("rest", [P, 2, CH])
        parts = sb("parts", [P, NQ, 3, CH], BF16)
        vt = sb("vt", [P, 2, 4, NQ, 4, VW])
        unused = sb("unused", [P, NST, 2], I32)
        tpsum = ps("tpsum", [P, DH, CH])
        qkpsum = ps("qkpsum", [P, 2, CH])
        vpsum = ps("vpsum", [P, 2, CH])

        weights_in = sem("weights_in")
        unused_set = sem("unused_set")
        const_set = sem("const_set")
        rweight_set = sem("rweight_set")
        ones_set = sem("ones_set")
        passed = sem("passed1")
        x_loaded = [sem(f"x_loaded{i}") for i in range(2)]
        x_stored = [sem(f"x_stored{i}") for i in range(2)]
        parts_stored = [sem(f"parts_stored{i}") for i in range(NQ)]
        v_stored = [sem(f"v_stored{i}") for i in range(2)]
        map_stored = sem("map_stored")
        dve_step = sem("dve_step")
        pool_step = sem("pool_step")
        mv_ready = sem("mv_ready")
        rstd_ready = sem("rstd_ready")
        xn_ready = sem("xn_ready")
        tp_ready = sem("tp_ready")
        xT0_ready = sem("xT0_ready")
        xT1_ready = sem("xT1_ready")
        qk_ready = sem("qk_ready")
        p1_ready = sem("p1_ready")
        rest_ready = sem("rest_ready")
        p2_ready = sem("p2_ready")
        p3_ready = sem("p3_ready")
        v_ready = sem("v_ready")
        v_taken = sem("v_taken")
        block = ctx.enter_context(nc.Block())

        RING = 2

        def chunks(eng, body):
            with eng.Fori(0, NC // 2 - 1) as i:
                body(2 * i, 0, True, i)
                body(2 * i + 1, 1, True, i)
            body(NC - 2, 0, True, NC // 2 - 1)
            body(NC - 1, 1, False, NC // 2 - 1)

        x_rows = ins["x"].rearrange("(c t p) d -> c p t d", c=NC, p=P)
        xn_rows = scratch["xn"].rearrange("(c t p) d -> c p t d", c=NC, p=P)

        @block.sync
        def _(sp):
            for i in range(2):
                sp.sem_inc(x_stored[i], 16)
                sp.sem_inc(v_stored[i], 16 * NQ)
                sp.dma_start(x_in[:, i], x_rows[i]).then_inc(x_loaded[i], 16)
            for q in range(NQ):
                sp.sem_inc(parts_stored[q], 16)
            sp.dma_start(w_vr[:, :, 0:D], ins["w_v"]).then_inc(weights_in, 16)
            sp.dma_start(w_vr[:, :, D:D + NE], ins["w_r"]).then_inc(weights_in, 16)
            sp.dma_start(rscale[:, :], ins["router_scale"]).then_inc(weights_in, 16)
            sp.dma_start(w_qk[:, :, :, :], ins["w_qk"]).then_inc(weights_in, 16)

            def stores(c, par, load):
                sp.wait_ge(xn_ready, c + 1)
                sp.dma_start(xn_rows[ds(c, 1)].rearrange("a p t d -> (a p) t d"), xn[:, par]).then_inc(x_stored[par], 16)
                if load:
                    sp.dma_start(x_in[:, par], x_rows[ds(c + 2, 1)].rearrange("a p t d -> (a p) t d")).then_inc(x_loaded[par], 16)
                for q in range(NQ):
                    sp.wait_ge(p3_ready, 4 * c + q + 1 + RING)
                    sp.dma_start(scratch["qk"][q].rearrange("a p t -> p a t")[:, :, ds(CH * c, CH)],
                                 parts[:, q]).then_inc(parts_stored[q], 16)
                sp.wait_ge(v_taken, 4 * c + 4 + RING)
                for q in range(NQ):
                    sp.dma_start(scratch["v"][q].rearrange("(t p) w -> p t w", p=P)[:, ds(4 * c, 4), :],
                                 vt[:, par, :, q].rearrange("p t h w -> p t (h w)")).then_inc(v_stored[par], 16)

            with sp.Fori(0, NC // 2 - 1) as i:
                stores(2 * i, 0, True)
                stores(2 * i + 1, 1, True)
            sp.wait_ge(unused_set, 2)
            sp.dma_start(scratch["map"].rearrange("(s p) c -> p s c", p=P), unused[:, :, :]).then_inc(map_stored, 16)
            stores(NC - 2, 0, False)
            stores(NC - 1, 1, False)
            for i in range(2):
                sp.wait_ge(x_stored[i], 16 + 16 * (NC // 2))
                sp.wait_ge(v_stored[i], 16 * NQ * (1 + NC // 2))
            for q in range(NQ):
                sp.wait_ge(parts_stored[q], 16 + 16 * NC)
            sp.wait_ge(map_stored, 16)

        @block.gpsimd
        def _(pool):
            pool.sem_inc(p3_ready, RING)
            pool.memset(ident[:, :], 0.0).then_inc(pool_step, 1)
            pool.memset(mhalf[:, :], -0.5).then_inc(const_set, 1)
            pool.wait_ge(pool_step, 1)
            pool.affine_select(out=ident[:, :], in_=ident[:, :], compare_op=ALU.not_equal, fill=1.0,
                               base=0, pattern=[[-1, P]], channel_multiplier=1).then_inc(const_set, 1)
            pool.memset(vt[:, :, :, :, :, :].rearrange("p b t q h w -> p (b t q h) w")[:, :, HD:VW], 1.0).then_inc(ones_set, 1)
            pool.wait_ge(const_set, 2)
            STEPS = 3

            def rstds(c, par):
                k = 1 + STEPS * c
                pool.wait_ge(mv_ready, c + 1)
                pool.sem_inc(passed, 1)
                pool.tensor_scalar(veps[:, par], mv[:, par, :, 1], LN_EPS, None, ALU.add).then_inc(pool_step, 1)
                pool.wait_ge(pool_step, k + 1)
                pool.tensor_tensor(rstd[:, par], veps[:, par], mhalf[:, 0:4], ALU.pow).then_inc(rstd_ready, 1)
                pool.wait_ge(rstd_ready, c + 1)
                pool.tensor_tensor(rsq[:, par], rstd[:, par], rstd[:, par], ALU.mult).then_inc(pool_step, 1)
                pool.wait_ge(pool_step, k + 2)
                pool.tensor_tensor(keep["msq"][:, ds(4 * c, 4)], rsq[:, par], mv[:, par, :, 1], ALU.mult).then_inc(pool_step, 1)

            rstds(0, 0)
            pool.iota(unused[:, :, 0], pattern=[[0, NST]], base=0, channel_multiplier=1).then_inc(unused_set, 1)
            pool.iota(unused[:, :, 1], pattern=[[P, NST]], base=2 * TOK, channel_multiplier=1).then_inc(unused_set, 1)

            def body(c, par, nxt, i):
                if nxt:
                    rstds(c + 1, 1 - par)
                for q in range(NQ):
                    pool.wait_ge(p2_ready, 4 * c + q + 1)
                    pool.tensor_tensor(parts[:, q, 2], rest[:, q % 2], parts[:, q, 1], ALU.subtract).then_inc(p3_ready, 1)

            chunks(pool, body)

        @block.vector
        def _(dve):
            dve.sem_inc(rest_ready, RING)
            dve.wait_ge(weights_in, 64)
            for dh in range(DH):
                last = dve.tensor_scalar(w_vr[:, dh, D:D + NE], w_vr[:, dh, D:D + NE], rscale[:, dh:dh + 1], None, ALU.mult)
            last.then_inc(rweight_set, 1)

            def normalise(c, par, i):
                dve.wait_ge(x_loaded[par], 16 * (i + 1))
                for t in range(4):
                    last = dve.bn_stats(stats[:, par, t], x_in[:, par, t])
                last.then_inc(dve_step, 1)
                dve.wait_ge(dve_step, c + 1)
                dve.sem_inc(passed, 1)
                for t in range(4):
                    last = dve.bn_aggr(mv[:, par, t], stats[:, par, t])
                last.then_inc(mv_ready, 1)
                dve.wait_ge(mv_ready, c + 1)
                dve.wait_ge(rstd_ready, c + 1)
                dve.wait_ge(x_stored[par], 16 * (i + 1))
                for t in range(4):
                    last = dve.tensor_scalar(xn[:, par, t], x_in[:, par, t], mv[:, par, t, 0:1],
                                             rstd[:, par, t:t + 1], ALU.subtract, ALU.mult)
                last.then_inc(xn_ready, 1)

            def evacuate(c, par):
                dve.wait_ge(tp_ready, 2 * c + 2)
                dve.tensor_copy(xT[:, par, 1], tpsum[:, 1]).then_inc(xT1_ready, 1)

            normalise(0, 0, 0)
            evacuate(0, 0)

            def body(c, par, nxt, i):
                if nxt:
                    normalise(c + 1, 1 - par, i + par)
                for q in range(NQ):
                    n = 4 * c + q
                    dve.wait_ge(p1_ready, n + 1)
                    dve.wait_ge(p3_ready, n + 1)
                    dve.tensor_tensor(rest[:, q % 2], qkpsum[:, q % 2], parts[:, q, 0], ALU.subtract).then_inc(rest_ready, 1)
                    dve.wait_ge(rest_ready, n + 1 + RING)
                    dve.tensor_copy(parts[:, q, 1], rest[:, q % 2]).then_inc(p2_ready, 1)
                if nxt:
                    evacuate(c + 1, 1 - par)

            chunks(dve, body)

        @block.scalar
        def _(act):
            act.sem_inc(v_taken, RING)

            def evacuate(c, par):
                act.wait_ge(tp_ready, 2 * c + 1)
                act.activation(xT[:, par, 0], tpsum[:, 0], ACT.Copy).then_inc(xT0_ready, 1)

            evacuate(0, 0)
            act.wait_ge(ones_set, 1)

            def body(c, par, nxt, i):
                for q in range(NQ):
                    n = 4 * c + q
                    act.wait_ge(qk_ready, n + 1)
                    act.wait_ge(parts_stored[q], 16 * (c + 1))
                    act.activation(parts[:, q, 0], qkpsum[:, q % 2], ACT.Copy).then_inc(p1_ready, 1)
                if nxt:
                    evacuate(c + 1, 1 - par)
                act.wait_ge(v_stored[par], 16 * NQ * (i + 1))
                for t in range(4):
                    act.wait_ge(v_ready, 4 * c + t + 1)
                    act.activation(vt[:, par, t].rearrange("p q h w -> p (q h) w")[:, :, 0:HD],
                                   vpsum[:, t % 2, 0:D].rearrange("p (g w) -> p g w", w=HD), ACT.Copy)
                    act.activation(keep["logits"][:, ds(4 * c + t, 1), :].rearrange("p a e -> p (a e)"),
                                   vpsum[:, t % 2, D:D + NE], ACT.Copy).then_inc(v_taken, 1)

            chunks(act, body)

        @block.tensor
        def _(pe):
            pe.wait_ge(const_set, 2)

            def transposes(c, par):
                pe.wait_ge(xn_ready, c + 1)
                for dh in range(DH):
                    for t in range(4):
                        last = pe.transpose(tpsum[:, dh, t * P:(t + 1) * P], xn[:, par, t, dh * P:(dh + 1) * P], ident[:, :])
                    last.then_inc(tp_ready, 1)

            transposes(0, 0)
            pe.wait_ge(weights_in, 64)
            pe.wait_ge(rweight_set, 1)

            def body(c, par, nxt, i):
                pe.wait_ge(xT0_ready, c + 1)
                pe.wait_ge(xT1_ready, c + 1)
                for q in range(NQ):
                    pe.wait_ge(rest_ready, 4 * c + q + 1)
                    for dh in range(DH):
                        last = pe.matmul(qkpsum[:, q % 2], w_qk[:, dh, q], xT[:, par, dh], start=dh == 0, stop=dh == DH - 1)
                    last.then_inc(qk_ready, 1)
                if nxt:
                    transposes(c + 1, 1 - par)
                for t in range(4):
                    pe.wait_ge(v_taken, 4 * c + t + 1)
                    for dh in range(DH):
                        last = pe.matmul(vpsum[:, t % 2, 0:D + NE], xT[:, par, dh, t * P:(t + 1) * P], w_vr[:, dh],
                                         start=dh == 0, stop=dh == DH - 1)
                    last.then_inc(v_ready, 1)

            chunks(pe, body)


def route(nc, ins, scratch, keep, heads):
    with ExitStack() as ctx:
        sb = lambda name, shape, dt=F32: ctx.enter_context(nc.sbuf_tensor(name, shape, dt))
        sem = lambda name: ctx.enter_context(nc.semaphore(name))
        counts = ctx.enter_context(nc.psum_tensor("counts", [P, 2, CH], F32))
        E3 = [P, NT, NE]
        msqe, rms = sb("msqe", [P, NT]), sb("rms", [P, NT])
        logit = sb("logit", E3)
        top = [sb(f"top{k}", [P, NT]) for k in range(2)]
        hit, key = sb("hit", E3), sb("key", E3)
        first = sb("first", [P, NT])
        chosen = [sb(f"chosen{k}", E3) for k in range(2)]
        masked = sb("masked", E3)
        expd, prob = sb("expd", E3), sb("prob", E3)
        esum = sb("esum", [P, NT])
        picked = sb("picked", E3)
        pk = [sb(f"pk{k}", [P, NT]) for k in range(2)]
        renorm, guard = sb("renorm", [P, NT]), sb("guard", [P, NT])
        escale = sb("escale", [P, NE])
        sk = sb("sk", [P, NT])
        rank_of, reset = sb("rank_of", [P, NE]), sb("reset", [P, NE, NT])
        both = sb("both", E3, BF16)
        tri, ones = sb("tri", [P, P], BF16), sb("ones", [P, P], BF16)
        cnt, run = sb("cnt", [P, NE, NT]), sb("run", [P, NE, NT])
        pos = sb("pos", [P, NE, NT])
        total, total_i = sb("total", [P, NE]), sb("total_i", [P, NE], I32)
        tiles_i, tiles = sb("tiles_i", [P, NE], I32), sb("tiles", [P, NE])
        ends, base = sb("ends", [P, NE]), sb("base", [P, NE])
        slot_f = sb("slot_f", [P, NT])
        tile_no, past = sb("tile_no", [1, NST, NE]), sb("past", [1, NST, NE])
        tile_f = sb("tile_f", [1, NST])
        scale_in = sem("scale_in")
        pool_set = sem("pool_set")
        rms_ready = sem("rms_ready")
        pool_step = sem("pool_step_r")
        dve_step = sem("dve_step_r")
        shifted = sem("shifted")
        exp_ready = sem("exp_ready")
        both_ready = sem("both_ready")
        counted = sem("counted")
        routed = sem("routed")
        block = ctx.enter_context(nc.Block())
        per_expert = lambda a: a.rearrange("p (t a) -> p t a", a=1).to_broadcast(E3)

        @block.sync
        def _(sp):
            sp.dma_start(escale[:, :], ins["expert_scale"].partition_broadcast(P)).then_inc(scale_in, 16)
            sp.wait_ge(scale_in, 16)
            load_quad(sp, scratch, heads, 0, 0)
            for q in range(NQ):
                sp.dma_start(heads["qs"][q][R_ALIBI:R_MAX, :, :], ins["c_q"][q]).then_inc(heads["const_in"], 16)
                sp.dma_start(heads["ks"][q][R_ALIBI:ROWS, :, :], ins["c_k"]).then_inc(heads["const_in"], 16)
            for hq in range(1, 3):
                load_quad(sp, scratch, heads, 0, hq)

        @block.gpsimd
        def _(pool):
            pool.tensor_scalar(msqe[:, :], keep["msq"][:, :], RMS_EPS, None, ALU.add).then_inc(pool_step, 1)
            pool.wait_ge(pool_step, 1)
            pool.tensor_tensor(rms[:, :], msqe[:, :], keep["mhalf"][:, 0:NT], ALU.pow).then_inc(rms_ready, 1)
            pool.iota(rank_of[:, :], pattern=[[-1, NE]], base=NE, channel_multiplier=0, allow_small_or_imprecise_dtypes=True).then_inc(pool_set, 1)
            pool.iota(tile_no[:, :, :], pattern=[[1, NST], [0, NE]], base=0, channel_multiplier=0, allow_small_or_imprecise_dtypes=True).then_inc(pool_set, 1)
            pool.memset(reset[:, :, :], 1.0).then_inc(pool_step, 1)
            pool.memset(ones[:, :], 1.0).then_inc(pool_set, 1)
            pool.wait_ge(pool_step, 2)
            pool.memset(reset[:, :, 0:1], 0.0).then_inc(pool_set, 1)
            pool.wait_ge(pool_set, 4)
            pool.affine_select(out=tri[:, :], in_=ones[:, :], compare_op=ALU.is_gt, fill=0.0,
                               base=0, pattern=[[1, P]], channel_multiplier=-1).then_inc(pool_set, 1)
            for k in range(2):
                for c in range(2):
                    pool.iota(keep["entries"][:, k, :, c], pattern=[[P, NT]], base=k * c * TOK, channel_multiplier=1).then_inc(pool_set, 1)
            mask = keep["mask"]
            pool.memset(mask[:, :], 0.0).then_inc(pool_step, 1)
            pool.wait_ge(pool_step, 3)
            pool.affine_select(out=mask[:, :], in_=mask[:, :], compare_op=ALU.is_ge, fill=NEG,
                               base=S - P, pattern=[[-1, S]], channel_multiplier=1).then_inc(pool_set, 1)

        @block.tensor
        def _(pe):
            pe.wait_ge(pool_set, 5)
            pe.wait_ge(both_ready, 1)
            rhs = both[:, :, :].rearrange("p t e -> p (t e)")
            pe.matmul(counts[:, 0, 0:NT * NE], tri[:, :], rhs, start=True, stop=True)
            pe.matmul(counts[:, 1, 0:NT * NE], ones[:, :], rhs, start=True, stop=True).then_inc(counted, 1)

        @block.scalar
        def _(act):
            act.wait_ge(shifted, 1)
            act.activation(expd[:, :, :], expd[:, :, :], ACT.Exp).then_inc(exp_ready, 1)

        @block.vector
        def _(dve):
            steps = [0]

            def then(ins_):
                ins_.then_inc(dve_step, 1)
                steps[0] += 1
                dve.wait_ge(dve_step, steps[0])

            dve.wait_ge(rms_ready, 1)
            dve.wait_ge(pool_set, 2)
            dve.wait_ge(scale_in, 16)
            then(dve.tensor_scalar(rms[:, :], rms[:, :], float(D) ** -0.5, None, ALU.mult))
            then(dve.tensor_tensor(logit[:, :, :], keep["logits"][:, :, :], per_expert(rms[:, :]), ALU.mult))
            src = logit
            rank3 = rank_of[:, :].rearrange("p (a e) -> p a e", a=1).to_broadcast(E3)
            for k in range(2):
                then(dve.tensor_reduce(top[k][:, :], src[:, :, :], AX_X, ALU.max))
                then(dve.tensor_tensor(hit[:, :, :], src[:, :, :], per_expert(top[k][:, :]), ALU.is_equal))
                then(dve.tensor_tensor(key[:, :, :], hit[:, :, :], rank3, ALU.mult))
                then(dve.tensor_reduce(first[:, :], key[:, :, :], AX_X, ALU.max))
                then(dve.tensor_tensor(chosen[k][:, :, :], rank3, per_expert(first[:, :]), ALU.is_equal))
                if k == 0:
                    then(dve.scalar_tensor_tensor(masked[:, :, :].rearrange("p t e -> p (t e)"),
                                                  chosen[0][:, :, :].rearrange("p t e -> p (t e)"), NEG,
                                                  logit[:, :, :].rearrange("p t e -> p (t e)"), ALU.mult, ALU.add))
                    src = masked
            dve.tensor_tensor(expd[:, :, :], logit[:, :, :], per_expert(top[0][:, :]), ALU.subtract).then_inc(shifted, 1)
            dve.tensor_tensor(both[:, :, :], chosen[0][:, :, :], chosen[1][:, :, :], ALU.add).then_inc(both_ready, 1)
            dve.wait_ge(exp_ready, 1)
            then(dve.tensor_reduce(esum[:, :], expd[:, :, :], AX_X, ALU.add))
            then(dve.reciprocal(esum[:, :], esum[:, :]))
            then(dve.tensor_tensor(prob[:, :, :], expd[:, :, :], per_expert(esum[:, :]), ALU.mult))
            for k in range(2):
                then(dve.tensor_tensor(picked[:, :, :], prob[:, :, :], chosen[k][:, :, :], ALU.mult))
                then(dve.tensor_reduce(pk[k][:, :], picked[:, :, :], AX_X, ALU.add))
            then(dve.tensor_tensor(renorm[:, :], pk[0][:, :], pk[1][:, :], ALU.add))
            then(dve.tensor_scalar(guard[:, :], renorm[:, :], 0.0, None, ALU.is_le))
            then(dve.tensor_tensor(renorm[:, :], renorm[:, :], guard[:, :], ALU.add))
            then(dve.reciprocal(renorm[:, :], renorm[:, :]))
            scale3 = escale[:, :].rearrange("p (a e) -> p a e", a=1).to_broadcast(E3)
            for k in range(2):
                then(dve.tensor_tensor(picked[:, :, :], scale3, chosen[k][:, :, :], ALU.mult))
                then(dve.tensor_reduce(sk[:, :], picked[:, :, :], AX_X, ALU.add))
                then(dve.tensor_tensor(sk[:, :], sk[:, :], renorm[:, :], ALU.mult))
                then(dve.tensor_tensor(keep["weight"][:, k], sk[:, :], pk[k][:, :], ALU.mult))
            dve.wait_ge(counted, 1)
            dve.wait_ge(pool_set, 4)
            view = lambda j: counts[:, j, 0:NT * NE].rearrange("p (t e) -> p e t", e=NE)
            then(dve.tensor_copy(cnt[:, :, :], view(1)))
            flat = lambda a: a[:, :, :].rearrange("p e t -> p (e t)")
            then(dve.tensor_tensor_scan(flat(run), flat(reset), flat(cnt), 0.0, ALU.mult, ALU.add))
            then(dve.tensor_scalar(total[:, :], run[:, :, NT - 1], float(P - 1), None, ALU.add))
            then(dve.tensor_copy(total_i[:, :], total[:, :]))
            then(dve.tensor_scalar(tiles_i[:, :], total_i[:, :], P.bit_length() - 1, None, ALU.arith_shift_right))
            then(dve.tensor_copy(tiles[:, :], tiles_i[:, :]))
            then(dve.tensor_tensor_scan(ends[:, :], reset[:, 0, 1:NE + 1], tiles[:, :], 0.0, ALU.mult, ALU.add))
            then(dve.tensor_tensor(base[:, :], ends[:, :], tiles[:, :], ALU.subtract))
            then(dve.tensor_scalar(base[:, :], base[:, :], float(P), None, ALU.mult))
            then(dve.tensor_tensor(pos[:, :, :], run[:, :, :], cnt[:, :, :], ALU.subtract))
            then(dve.tensor_tensor(pos[:, :, :], pos[:, :, :], view(0), ALU.add))
            then(dve.tensor_tensor(pos[:, :, :], pos[:, :, :], base[:, :].rearrange("p (e a) -> p e a", a=1).to_broadcast([P, NE, NT]), ALU.add))
            for k in range(2):
                then(dve.tensor_tensor(picked[:, :, :], pos[:, :, :].rearrange("p e t -> p t e"), chosen[k][:, :, :], ALU.mult))
                then(dve.tensor_reduce(slot_f[:, :], picked[:, :, :], AX_X, ALU.add))
                then(dve.tensor_copy(keep["slot"][:, k], slot_f[:, :]))
            then(dve.tensor_tensor(past[:, :, :], tile_no[:, :, :], ends[0:1, :].rearrange("p (a e) -> p a e", a=1).to_broadcast([1, NST, NE]), ALU.is_ge))
            then(dve.tensor_reduce(tile_f[:, :], past[:, :, :], AX_X, ALU.add))
            dve.tensor_scalar(keep["tile_expert"][:, :], tile_f[:, :], float(NE - 1), None, ALU.min).then_inc(routed, 1)
            dve.wait_ge(routed, 1)
            dve.wait_ge(pool_set, 10)


def attend(nc, ins, scratch, keep, heads):
    with ExitStack() as ctx:
        sb = lambda name, shape, dt=F32: ctx.enter_context(nc.sbuf_tensor(name, shape, dt))
        sem = lambda name: ctx.enter_context(nc.semaphore(name))
        qs, ks, vs = heads["qs"], heads["ks"], heads["vs"]
        probs = sb("probs", [P, PRING, 4, CH])
        junk = sb("junk", [P, 2, S], BF16)
        maxima = sb("maxima", [P, 2, 4, KT])
        mrest = sb("mrest", [4 * KT, P])
        mparts = sb("mparts", [4 * KT, 2, 3, P], BF16)
        entries = sb("entries_now", [P, 2, 2, 2, 2], I32)
        slots = sb("slots", [P, 2, 2, 2], I32)
        mpsum = ctx.enter_context(nc.psum_tensor("mpsum", [P, 2, S], F32))
        spsum = ctx.enter_context(nc.psum_tensor("spsum", [P, 2, CH], F32))
        cpsum = ctx.enter_context(nc.psum_tensor("cpsum", [P, 2, CH], F32))

        stack_in, const_in, v_in = heads["stack_in"], heads["const_in"], heads["v_in"]
        mrow_in = [sem(f"mrow_in{i}") for i in range(NQ)]
        cleared = sem("cleared")
        passed = sem("passed3")
        m_ready = sem("m_ready")
        m_taken = sem("m_taken")
        max_step = sem("max_step")
        max_split = sem("max_split")
        s_ready = sem("s_ready")
        exp_done = sem("exp_done")
        masked = sem("masked")
        pv_done = sem("pv_done")
        ctx_taken = sem("ctx_taken")
        entries_in = [sem(f"entries_in{i}") for i in range(2)]
        entries_out = [sem(f"entries_out{i}") for i in range(2)]
        block = ctx.enter_context(nc.Block())
        RING = 2

        def wait_apart(eng, sem, value):
            eng.wait_ge(sem, value)
            eng.sem_inc(passed, 1)

        def steps(eng, body):
            with eng.Fori(0, B - 1) as b:
                for hq in range(NQ):
                    body(NQ * b + hq, b, hq, lambda j: True)
            for hq in range(NQ):
                body(NQ * (B - 1) + hq, B - 1, hq, lambda j, hq=hq: hq + j < NQ)

        def quad(b, hq, j):
            return b + (hq + j) // NQ, (hq + j) % NQ

        @block.sync
        def _(sp):
            def maxima_rows(n, hq):
                sp.wait_ge(max_split, n + 1)
                for j in range(3):
                    sp.dma_start(qs[hq][R_MAX + j:R_MAX + j + 1, :, :], mparts[:, hq % 2, j, :]).then_inc(mrow_in[hq], 16)

            def tile_entries(t, par):
                sp.dma_start(entries[:, par], keep["entries"][:, :, ds(2 * t, 2), :]).then_inc(entries_in[par], 16)
                sp.dma_start(slots[:, par], keep["slot"][:, :, ds(2 * t, 2)]).then_inc(entries_in[par], 16)

            for t in range(2):
                tile_entries(t, t)
            maxima_rows(0, 0)
            for e in range(NE):
                sp.dma_start(keep["w_gu"][:, e * DH:(e + 1) * DH], ins["w_gu"][:, e * DH:(e + 1) * DH]).then_inc(keep["w_gu_in"], 16)

            def body(t, b, hq, has):
                par = hq % 2
                if has(3):
                    sp.wait_ge(pv_done, PRING + NU * t)
                    load_quad(sp, scratch, heads, *quad(b, hq, 3))
                if has(1):
                    maxima_rows(t + 1, (hq + 1) % NQ)
                sp.wait_ge(entries_out[par], 64 * (2 * b + hq // 2 + 1))
                if has(2):
                    tile_entries(t + 2, par)

            steps(sp, body)
            for i in range(2):
                sp.wait_ge(entries_out[i], 64 * (B * NQ // 2))

        @block.gpsimd
        def _(pool):
            def body(t, b, hq, has):
                par = hq % 2
                wait_apart(pool, entries_in[par], 32 * (2 * b + hq // 2 + 1))
                for i in range(2):
                    for k in range(2):
                        pool.indirect_dma_start(scratch["map"], bass.IndirectOffsetOnAxis(ap=slots[:, par, k, i:i + 1].bitcast(U32), axis=0),
                                                entries[:, par, k, i, :], None).then_inc(entries_out[par], 16)
                for j in range(1, NU + 1):
                    if j == NU and not has(1):
                        continue
                    mask_unit(NU * t + j, j % NU)

            def mask_unit(n, u):
                if not DIAG[u]:
                    return
                wait_apart(pool, exp_done, 4 * n + 4 + RING)
                for c in DIAG[u]:
                    part = probs[:, u % PRING, :, c:c + P]
                    pool.affine_select(out=part, in_=part, compare_op=ALU.is_ge, fill=0.0, base=0,
                                       pattern=[[0, 4], [1, P]], channel_multiplier=-1).then_inc(masked, 1)

            mask_unit(0, 0)
            steps(pool, body)

        @block.vector
        def _(dve):
            dve.sem_inc(m_taken, RING)
            dve.memset(cpsum[:, :, :], 0.0).then_inc(cleared, 1)

            def item(t, hq, k):
                n = NI * t + k
                slot = (NI * hq + k) % RING
                dve.wait_ge(m_taken, n + 1)
                wait_apart(dve, m_ready, n + 1)
                if k < NI - 1:
                    h, qt = ITEMS[k]
                    w = (qt + 1) * P
                    last = dve.tensor_tensor_reduce(junk[:, slot, 0:w], mpsum[:, slot, 0:w], keep["mask"][:, S - w:S], 1.0, 3 * NEG,
                                                    ALU.add, ALU.max, maxima[:, hq % 2, h, qt:qt + 1])
                    last.then_inc(m_taken, 1)
                    return
                mT = mpsum[0:4 * KT, slot, 0:P]
                parts = mparts[:, hq % 2]
                dve.tensor_scalar(parts[:, 0], mT, -1.0, None, ALU.mult).then_inc(max_step, 1)
                dve.wait_ge(max_step, 3 * t + 1)
                dve.scalar_tensor_tensor(mrest[:, :], mT, -1.0, parts[:, 0], ALU.mult, ALU.subtract).then_inc(m_taken, 1)
                dve.wait_ge(m_taken, n + 1 + RING)
                dve.tensor_copy(parts[:, 1], mrest[:, :]).then_inc(max_step, 1)
                dve.wait_ge(max_step, 3 * t + 2)
                dve.tensor_tensor(parts[:, 2], mrest[:, :], parts[:, 1], ALU.subtract).then_inc(max_step, 1)
                dve.wait_ge(max_step, 3 * t + 3)
                dve.sem_inc(max_split, 1)

            for k in range(NI):
                item(0, 0, k)
            for k in range(LEAD):
                item(1, 1, k)

            def body(t, b, hq, has):
                for slot in SLOT_ITEMS:
                    for j, k in slot:
                        if has(j):
                            item(t + j, (hq + j) % NQ, k)

            steps(dve, body)

        @block.scalar
        def _(act):
            act.sem_inc(exp_done, RING)

            def exps(n, u, heads):
                for h in heads:
                    m = 4 * n + h
                    act.wait_ge(s_ready, m + 1)
                    if h == 0:
                        act.wait_ge(pv_done, n + 1)
                    act.activation(probs[:, u % PRING, h], spsum[:, h % 2], ACT.Exp, scale=SCALE).then_inc(exp_done, 1)

            exps(0, 0, range(4))

            def body(t, b, hq, has):
                for u in range(1, NU):
                    exps(NU * t + u, u, range(4))
                if has(1):
                    exps(NU * t + NU, 0, range(4))
                act.wait_ge(pv_done, NU * t + NU + PRING)
                act.activation(keep["ctxT"][:, ds(t, 1), 0:CH].rearrange("p a c -> p (a c)"), cpsum[:, 0], ACT.Copy)
                act.activation(keep["ctxT"][:, ds(t, 1), CH:S].rearrange("p a c -> p (a c)"), cpsum[:, 1], ACT.Copy).then_inc(ctx_taken, 1)

            steps(act, body)

        @block.tensor
        def _(pe):
            pe.sem_inc(pv_done, PRING)
            pe.sem_inc(ctx_taken, 1)
            pe.wait_ge(cleared, 1)
            pe.wait_ge(const_in, 16 * 2 * NQ)

            def item(t, b, hq, k):
                n = NI * t + k
                slot = (NI * hq + k) % RING
                if k == 0:
                    pe.wait_ge(stack_in[hq], 16 * STACK_DMAS * (b + 1))
                pe.wait_ge(m_taken, n + 1)
                if k < NI - 1:
                    h, qt = ITEMS[k]
                    w = (qt + 1) * P
                    for c in range(0, w, CH):
                        e = min(w, c + CH)
                        last = pe.matmul(mpsum[:, slot, c:e], qs[hq][0:R_MAX, h, qt * P:(qt + 1) * P], ks[hq][0:R_MAX, h, c:e],
                                         start=True, stop=True)
                    last.then_inc(m_ready, 1)
                else:
                    pe.wait_ge(m_taken, n + RING)
                    pe.transpose(mpsum[0:4 * KT, slot, 0:P], maxima[:, hq % 2].rearrange("p h q -> p (h q)"), keep["ident"][:, :]).then_inc(m_ready, 1)

            def scores(n, hq, u, h):
                m = 4 * n + h
                pe.wait_ge(exp_done, m + 1)
                for c, kt, q0, w in UNITS[u]:
                    last = pe.matmul(spsum[:, h % 2, c:c + w], ks[hq][:, h, kt * P:(kt + 1) * P], qs[hq][:, h, q0:q0 + w],
                                     start=True, stop=True)
                last.then_inc(s_ready, 1)

            def weighted(n, t, b, hq, u, half):
                if half == 0:
                    pe.wait_ge(exp_done, 4 * n + 4 + RING)
                    if u == 0:
                        pe.wait_ge(v_in[hq], 16 * (b + 1))
                        pe.wait_ge(ctx_taken, t + 1)
                elif DIAG[u]:
                    pe.wait_ge(masked, MASKED[NU] * t + MASKED[u + 1])
                for c, kt, q0, w in PV[u][half]:
                    bank = q0 // CH
                    for h in range(4):
                        last = pe.matmul(cpsum[32 * h:32 * h + VW, bank, q0 - bank * CH:q0 - bank * CH + w], vs[hq][:, kt, h], probs[:, u % PRING, h, c:c + w],
                                         start=kt == 0 and half == 0, stop=kt == (3 if bank == 0 else 7), tile_position=(0, 32 * h), skip_group_check=True)
                if half == 1:
                    last.then_inc(pv_done, 1)

            for k in range(NI):
                item(0, 0, 0, k)
            for k in range(LEAD):
                item(1, 0, 1, k)
                if k == LEAD - 4:
                    pe.wait_ge(mrow_in[0], 48)
                if k >= LEAD - 4:
                    scores(0, 0, 0, k - (LEAD - 4))

            def body(t, b, hq, has):
                for j in range(1, NU + 1):
                    u, n = j % NU, NU * t + j
                    b1, hq1 = quad(b, hq, 1) if j == NU else (b, hq)
                    for h in range(4):
                        if j < NU or has(1):
                            if u == 0 and h == 0:
                                pe.wait_ge(mrow_in[hq1], 48 * (b1 + 1))
                            scores(n, hq1, u, h)
                        for ahead, k in SLOT_ITEMS[4 * (j - 1) + h]:
                            if has(ahead):
                                item(t + ahead, *quad(b, hq, ahead), k)
                        if h % 2 == 1:
                            weighted(n - 1, t, b, hq, j - 1, h // 2)

            steps(pe, body)


def experts(nc, ins, scratch, keep, last_weights):
    RR = 4
    AHEAD = 6
    with ExitStack() as ctx:
        sb = lambda name, shape, dt=F32: ctx.enter_context(nc.sbuf_tensor(name, shape, dt))
        sem = lambda name: ctx.enter_context(nc.semaphore(name))
        w_gu = keep["w_gu"]
        w_down = sb("w_down", [P, NE * DH, D])
        rows = sb("rows", [P, RR, D])
        from_row = sb("from_row", [P, RR, 2], I32)
        to_row = sb("to_row", [P, RR, 2], I32)
        xT = sb("xTs", [P, 2, DH, P])
        gate = sb("gate", [P, 2, HID])
        hid = sb("hid", [P, 2, HID])
        hT = sb("hT", [P, 2, DH, P])
        y = sb("y", [P, 2, D])
        tp = ctx.enter_context(nc.psum_tensor("tp", [P, 2, CH], F32))
        gu = ctx.enter_context(nc.psum_tensor("gu", [P, 2, CH], F32))
        hp = ctx.enter_context(nc.psum_tensor("hp", [P, 2, CH], F32))
        yp = ctx.enter_context(nc.psum_tensor("yp", [P, 2, CH], F32))
        w_in = sem("w_in")
        from_in = [sem(f"from_in{i}") for i in range(RR)]
        to_in = [sem(f"to_in{i}") for i in range(RR)]
        rows_in = [sem(f"rows_in{i}") for i in range(RR)]
        y_out = [sem(f"y_out{i}") for i in range(RR)]
        y_free, passed = sem("y_free"), sem("passed4")
        tp_ready, xT_ready = sem("tps_ready"), sem("xTs_ready")
        gu_ready, gate_ready, hid_ready = sem("gu_ready"), sem("gate_ready"), sem("hid_ready")
        hp_ready, hT_ready = sem("hp_ready"), sem("hT_ready")
        yp_ready, y_ready = sem("yp_ready"), sem("y_ready")
        block = ctx.enter_context(nc.Block())
        slot_map = scratch["map"].rearrange("(s p) c -> s p c", p=P)

        def tiles(eng, body):
            with eng.Fori(0, NST // 2) as i:
                for par in range(2):
                    body(2 * i + par, par, i)

        @block.sync
        def _(sp):
            sp.sem_inc(tp_ready, RR)
            sp.sem_inc(y_free, RR)

            def from_rows(s, m):
                sp.wait_ge(tp_ready, s + 1)
                sp.dma_start(from_row[:, m], slot_map[ds(s, 1)].rearrange("a p c -> (a p) c")).then_inc(from_in[m], 16)

            def to_rows(s, m):
                sp.wait_ge(y_free, s + 1)
                sp.dma_start(to_row[:, m], slot_map[ds(s, 1)].rearrange("a p c -> (a p) c")).then_inc(to_in[m], 16)

            for m in range(RR):
                from_rows(m, m)
            for e in range(NE):
                sp.dma_start(w_down[:, e * DH:(e + 1) * DH], ins["w_down"][:, e * DH:(e + 1) * DH]).then_inc(w_in, 16)
            sp.dma_start(last_weights["w_o"][:, :, :], ins["w_o"]).then_inc(last_weights["in"], 16)
            sp.dma_start(last_weights["bias"][:, :], ins["bo"].partition_broadcast(P)).then_inc(last_weights["in"], 16)
            with sp.Fori(0, NST // RR - 1) as i:
                for m in range(RR):
                    from_rows(RR * (i + 1) + m, m)
                    to_rows(RR * i + m, m)
            for m in range(RR):
                to_rows(NST - RR + m, m)

        @block.gpsimd
        def _(pool):
            def gather(s, m, i):
                pool.wait_ge(from_in[m], 16 * (i + 1))
                pool.sem_inc(passed, 1)
                pool.indirect_dma_start(rows[:, m], None, scratch["xn"],
                                        bass.IndirectOffsetOnAxis(ap=from_row[:, m, 0:1].bitcast(U32), axis=0)).then_inc(rows_in[m], 16)

            def scatter(s, m, i, first=False):
                pool.wait_ge(to_in[m], 16 * (i + 1))
                pool.wait_ge(y_ready, s + 1)
                if not first:
                    pool.wait_ge(y_out[(m - 1) % RR], 16 * (i + 1 - (m == 0)))
                    pool.sem_inc(y_free, 1)
                pool.indirect_dma_start(scratch["y"], bass.IndirectOffsetOnAxis(ap=to_row[:, m, 1:2].bitcast(U32), axis=0),
                                        y[:, m % 2], None).then_inc(y_out[m], 16)

            for s in range(AHEAD):
                gather(s, s % RR, s // RR)
            scatter(0, 0, 0, first=True)
            gather(AHEAD, AHEAD % RR, AHEAD // RR)
            turns = (NST - 1 - AHEAD) // RR
            with pool.Fori(0, turns) as i:
                for j in range(1, RR + 1):
                    scatter(RR * i + j, j % RR, i + j // RR)
                    gather(RR * i + j + AHEAD, (j + AHEAD) % RR, i + (j + AHEAD) // RR)
            for s in range(RR * turns + 1, NST):
                scatter(s, s % RR, s // RR)
                if s + AHEAD < NST:
                    gather(s + AHEAD, (s + AHEAD) % RR, (s + AHEAD) // RR)
            for m in range(RR):
                pool.wait_ge(y_out[m], 16 * (NST // RR))

        @block.scalar
        def _(act):
            def xT_copy(s, par):
                act.wait_ge(tp_ready, s + 1 + RR)
                act.activation(xT[:, par].rearrange("p a t -> p (a t)"), tp[:, par, 0:D], ACT.Copy).then_inc(xT_ready, 1)

            def gelu(s, par):
                act.wait_ge(gu_ready, s + 1)
                act.activation(gate[:, par], gu[:, par, 0:HID], ACT.Gelu_apprx_tanh).then_inc(gate_ready, 1)

            def store(s, par):
                act.wait_ge(yp_ready, s + 1)
                act.wait_ge(y_free, s + 1 + RR - 2)
                act.activation(y[:, par], yp[:, par, 0:D], ACT.Copy).then_inc(y_ready, 1)

            xT_copy(0, 0)
            gelu(0, 0)
            xT_copy(1, 1)
            gelu(1, 1)
            xT_copy(2, 0)
            with act.Fori(0, NST // 2 - 2) as i:
                for par in range(2):
                    s = 2 * i + 2 + par
                    gelu(s, par)
                    xT_copy(s + 1, 1 - par)
                    store(s - 2, par)
            gelu(NST - 2, 0)
            xT_copy(NST - 1, 1)
            store(NST - 4, 0)
            gelu(NST - 1, 1)
            for s in range(NST - 3, NST):
                store(s, s % 2)

        @block.vector
        def _(dve):
            def body(s, par, i):
                dve.wait_ge(gate_ready, s + 1)
                dve.tensor_tensor(hid[:, par], gu[:, par, HID:2 * HID], gate[:, par], ALU.mult).then_inc(hid_ready, 1)
                dve.wait_ge(hp_ready, s + 1)
                dve.tensor_copy(hT[:, par].rearrange("p a t -> p (a t)"), hp[:, par, 0:HID]).then_inc(hT_ready, 1)

            tiles(dve, body)

        @block.tensor
        def _(pe):
            pe.wait_ge(keep["w_gu_in"], 16 * NE)

            def rows_T(s, m, i):
                pe.wait_ge(rows_in[m], 16 * (i + 1))
                for dh in range(DH):
                    last = pe.transpose(tp[:, m % 2, dh * P:(dh + 1) * P], rows[:, m, dh * P:(dh + 1) * P], keep["ident"][:, :])
                last.then_inc(tp_ready, 1)

            def gate_up(s, par):
                e = pe.value_load(keep["tile_expert"][0:1, ds(s, 1)], min_val=0, max_val=NE - 1)
                pe.wait_ge(xT_ready, s + 1)
                for dh in range(DH):
                    last = pe.matmul(gu[:, par], xT[:, par, dh], w_gu[:, ds(e * DH + dh, 1)].rearrange("p a c -> p (a c)"),
                                     start=dh == 0, stop=dh == DH - 1)
                last.then_inc(gu_ready, 1)

            def hidden_T(s, par):
                pe.wait_ge(hid_ready, s + 1)
                for dh in range(DH):
                    last = pe.transpose(hp[:, par, dh * P:(dh + 1) * P], hid[:, par, dh * P:(dh + 1) * P], keep["ident"][:, :])
                last.then_inc(hp_ready, 1)

            def down(s, par):
                e = pe.value_load(keep["tile_expert"][0:1, ds(s, 1)], min_val=0, max_val=NE - 1)
                pe.wait_ge(hT_ready, s + 1)
                for dh in range(DH):
                    last = pe.matmul(yp[:, par, 0:D], hT[:, par, dh], w_down[:, ds(e * DH + dh, 1)].rearrange("p a c -> p (a c)"),
                                     start=dh == 0, stop=dh == DH - 1)
                last.then_inc(yp_ready, 1)

            rows_T(0, 0, 0)
            gate_up(0, 0)
            rows_T(1, 1, 0)
            gate_up(1, 1)
            hidden_T(0, 0)
            rows_T(2, 2, 0)
            pe.wait_ge(w_in, 16 * NE)
            with pe.Fori(0, NST // RR - 1) as i:
                for j in range(2, 2 + RR):
                    s, par = RR * i + j, j % 2
                    gate_up(s, par)
                    hidden_T(s - 1, 1 - par)
                    rows_T(s + 1, (j + 1) % RR, i + (j + 1) // RR)
                    down(s - 2, par)
            gate_up(NST - 2, 0)
            hidden_T(NST - 3, 1)
            rows_T(NST - 1, RR - 1, NST // RR - 1)
            down(NST - 4, 0)
            gate_up(NST - 1, 1)
            hidden_T(NST - 2, 0)
            down(NST - 3, 1)
            hidden_T(NST - 1, 1)
            down(NST - 2, 0)
            pe.wait_ge(y_ready, NST - 2)
            down(NST - 1, 1)


def combine(nc, ins, scratch, keep, last_weights, out):
    with ExitStack() as ctx:
        sb = lambda name, shape, dt=F32: ctx.enter_context(nc.sbuf_tensor(name, shape, dt))
        sem = lambda name: ctx.enter_context(nc.semaphore(name))
        NP, PB = NT // 2, KT // 2
        LOADS = 4
        w_o, bias, w_in = last_weights["w_o"], last_weights["bias"], last_weights["in"]
        sums = sb("sums", [P, PB, NQ, 2 * P])
        xr = sb("xr", [P, PB, 2, D])
        wts = sb("wts", [P, PB, 2, 2])
        inv = sb("inv", [P, 2, NH])
        ctxn = sb("ctxn", [P, 2, NH, HD])
        ctxnT = sb("ctxnT", [P, 2, 2, D])
        yk = sb("yk", [P, PB, 2, 2, D])
        xb = sb("xb", [P, 2, 2, D])
        acc = sb("acc", [P, 3, 2, D])
        done = sb("done", [P, 2, 2, D])
        sumsT = ctx.enter_context(nc.psum_tensor("sumsT", [P, 2, CH], F32))
        backT = ctx.enter_context(nc.psum_tensor("backT", [P, 2, CH], F32))
        proj = ctx.enter_context(nc.psum_tensor("proj", [P, 2, CH], F32))
        loaded = [sem(f"loaded{i}") for i in range(PB)]
        out_done = [sem(f"out_done{i}") for i in range(2)]
        sumsT_ready, inv_ready, norm_ready = sem("sumsT_ready"), sem("inv_ready"), sem("norm_ready")
        staged = sem("staged")
        backT_ready, ctxnT_ready, proj_ready = sem("backT_ready"), sem("ctxnT_ready"), sem("proj_ready")
        xb_ready, acc_ready, one_ready, pair_done = sem("xb_ready"), sem("acc_ready"), sem("one_ready"), sem("pair_done")
        block = ctx.enter_context(nc.Block())
        x_rows = ins["x"].rearrange("(g p) d -> p g d", p=P)
        y_rows = [scratch["y"][k * TOK:(k + 1) * TOK].rearrange("(g p) d -> p g d", p=P) for k in range(2)]
        out_rows = out.rearrange("(g p) d -> p g d", p=P)
        RING = 2

        def pairs(eng, body):
            with eng.Fori(0, B - 1) as b:
                for p in range(1, PB + 1):
                    body(b, p)
            for p in range(1, PB + 1):
                body(B - 1, p)

        def exists(b, p):
            return not isinstance(b, int) or PB * b + p < NP

        @block.sync
        def _(sp):
            for i in range(2):
                sp.sem_inc(out_done[i], 16)

            def load(b, p):
                g = 2 * (PB * b + p)
                sp.dma_start(xr[:, p], x_rows[:, ds(g, 2), :]).then_inc(loaded[p], 16)
                for k in range(2):
                    sp.dma_start(yk[:, p, k], y_rows[k][:, ds(g, 2), :]).then_inc(loaded[p], 16)
                sp.dma_start(wts[:, p], keep["weight"][:, :, ds(g, 2)]).then_inc(loaded[p], 16)

            def store(b, p):
                sp.wait_ge(pair_done, PB * b + p + 1 + RING)
                sp.dma_start(out_rows[:, ds(2 * (PB * b + p), 2), :], done[:, p % 2]).then_inc(out_done[p % 2], 16)

            for p in range(PB):
                load(0, p)
            with sp.Fori(0, B - 1) as b:
                for p in range(PB):
                    store(b, p)
                    load(b + 1, p)
            for p in range(PB):
                store(B - 1, p)
            for i in range(2):
                sp.wait_ge(out_done[i], 16 + 16 * (NP // 2))

        @block.gpsimd
        def _(pool):
            pool.wait_ge(w_in, 32)
            with pool.Fori(0, B) as b:
                for p in range(PB):
                    pool.wait_ge(loaded[p], 16 * LOADS * (b + 1))
                    pool.wait_ge(pair_done, PB * b + p + 1)
                    pool.tensor_tensor(xb[:, p % 2], xr[:, p], bias[:, :].rearrange("p (a d) -> p a d", a=1).to_broadcast([P, 2, D]), ALU.add).then_inc(xb_ready, 1)

        @block.tensor
        def _(pe):
            pe.sem_inc(norm_ready, 1)
            pe.wait_ge(w_in, 32)

            def turn(b, p):
                p, b = p % PB, b + p // PB
                pe.wait_ge(staged, PB * b + p + 1)
                pe.wait_ge(norm_ready, PB * b + p + 1)
                for t in range(2):
                    for q in range(NQ):
                        last = pe.transpose(sumsT[:, t, P * q:P * (q + 1)], sums[:, p, q, P * t:P * (t + 1)], keep["ident"][:, :])
                last.then_inc(sumsT_ready, 1)

            def turn_back(b, p):
                p, b = p % PB, b + p // PB
                pe.wait_ge(norm_ready, PB * b + p + 2)
                for t in range(2):
                    for dh in range(DH):
                        last = pe.transpose(backT[:, p % 2, D * t + P * dh:D * t + P * (dh + 1)],
                                            ctxn[:, t].rearrange("p h w -> p (h w)")[:, P * dh:P * (dh + 1)], keep["ident"][:, :])
                last.then_inc(backT_ready, 1)

            def project_pair(b, p):
                p, b = p % PB, b + p // PB
                pe.wait_ge(ctxnT_ready, PB * b + p + 1)
                for t in range(2):
                    for dh in range(DH):
                        last = pe.matmul(proj[:, p % 2, D * t:D * (t + 1)], ctxnT[:, p % 2, t, P * dh:P * (dh + 1)], w_o[:, dh],
                                         start=dh == 0, stop=dh == DH - 1)
                last.then_inc(proj_ready, 1)

            turn(0, 0)
            turn_back(0, 0)
            turn(0, 1)

            def body(b, p):
                if exists(b, p):
                    turn_back(b, p)
                    if exists(b, p + 1):
                        turn(b, p + 1)
                project_pair(b, p - 1)

            pairs(pe, body)

        @block.scalar
        def _(act):
            def stage(b, p):
                p, b = p % PB, b + p // PB
                act.activation(sums[:, p], keep["ctxT"][:, ds(NQ * b, NQ), 2 * P * p:2 * P * (p + 1)], ACT.Copy).then_inc(staged, 1)

            stage(0, 0)
            stage(0, 1)

            def turned(b, p):
                    act.wait_ge(backT_ready, PB * b + p + 1)
                    act.wait_ge(pair_done, PB * b + p + 1)
                    act.activation(ctxnT[:, p % 2].rearrange("p t c -> p (t c)"), backT[:, p % 2], ACT.Copy).then_inc(ctxnT_ready, 1)
                    if exists(b, p + 2):
                        stage(b, p + 2)

            with act.Fori(0, B - 1) as b:
                for p in range(PB):
                    turned(b, p)
            for p in range(PB):
                turned(B - 1, p)

        @block.vector
        def _(dve):
            dve.sem_inc(pair_done, RING)
            dve.wait_ge(w_in, 32)

            def normalise(b, p):
                p, b = p % PB, b + p // PB
                n = PB * b + p
                dve.wait_ge(sumsT_ready, n + 1)
                heads = sumsT[:, :, :].rearrange("p t (h w) -> p t h w", w=32)
                for t in range(2):
                    dve.reciprocal(inv[:, t], heads[:, t, :, HD]).then_inc(inv_ready, 1)
                if not isinstance(b, int) or n > 0:
                    dve.wait_ge(backT_ready, n)
                dve.wait_ge(inv_ready, 2 * n + 2)
                for t in range(2):
                    last = dve.tensor_tensor(ctxn[:, t], heads[:, t, :, 0:HD],
                                             inv[:, t].rearrange("p (h a) -> p h a", a=1).to_broadcast([P, NH, HD]), ALU.mult)
                last.then_inc(norm_ready, 1)

            def total_up(b, p):
                p, b = p % PB, b + p // PB
                n = PB * b + p
                dve.wait_ge(proj_ready, n + 1)
                dve.wait_ge(xb_ready, n + 1)
                dve.tensor_tensor(acc[:, 0].rearrange("p t d -> p (t d)"), proj[:, p % 2], xb[:, p % 2].rearrange("p t d -> p (t d)"), ALU.add).then_inc(acc_ready, 1)
                dve.wait_ge(acc_ready, n + 1)
                dve.wait_ge(loaded[p], 16 * LOADS * (b + 1))
                for t in range(2):
                    dve.scalar_tensor_tensor(acc[:, 1, t], yk[:, p, 0, t], wts[:, p, 0, t:t + 1], acc[:, 0, t], ALU.mult, ALU.add).then_inc(one_ready, 1)
                dve.wait_ge(out_done[p % 2], 16 * (PB // 2 * b + p // 2 + 1))
                for t in range(2):
                    dve.wait_ge(one_ready, 2 * n + t + 1)
                    last = dve.scalar_tensor_tensor(done[:, p % 2, t], yk[:, p, 1, t], wts[:, p, 1, t:t + 1], acc[:, 1, t], ALU.mult, ALU.add)
                last.then_inc(pair_done, 1)

            normalise(0, 0)
            normalise(0, 1)

            def body(b, p):
                if exists(b, p + 1):
                    normalise(b, p + 1)
                total_up(b, p - 1)

            pairs(dve, body)


def build(nc, ins, out):
    with ExitStack() as ctx:
        sb = lambda name, shape, dt=F32: ctx.enter_context(nc.sbuf_tensor(name, shape, dt))
        keep = {
            "ident": sb("ident", [P, P]),
            "mhalf": sb("mhalf", [P, NT]),
            "mask": sb("mask", [P, S]),
            "msq": sb("msq", [P, NT]),
            "logits": sb("logits", [P, NT, NE]),
            "weight": sb("weight", [P, 2, NT]),
            "slot": sb("slot", [P, 2, NT], I32),
            "entries": sb("entries", [P, 2, NT, 2], I32),
            "tile_expert": sb("tile_expert", [1, NST], I32),
            "w_gu": sb("w_gu", [P, NE * DH, 2 * HID]),
            "w_gu_in": ctx.enter_context(nc.semaphore("w_gu_in")),
            "ctxT": sb("ctxT", [P, B * NQ, S]),
        }
        scratch = {
            "xn": nc.dram_tensor("xn_rows", [TOK, D], F32).ap(),
            "qk": nc.dram_tensor("qk_parts", [NQ, 3, P, TOK], BF16).ap(),
            "v": nc.dram_tensor("v_rows", [NQ, TOK, 4 * VW], F32).ap(),
            "map": nc.dram_tensor("slot_map", [NST * P, 2], I32).ap(),
            "y": nc.dram_tensor("expert_rows", [2 * TOK + NST * P, D], F32).ap(),
        }
        project(nc, ins, scratch, keep)
        with ExitStack() as held:
            heads = head_buffers(nc, held)
            route(nc, ins, scratch, keep, heads)
            attend(nc, ins, scratch, keep, heads)
        last_weights = {"w_o": sb("w_o", [P, DH, D]), "bias": sb("bias", [P, D]),
                        "in": ctx.enter_context(nc.semaphore("wo_in"))}
        experts(nc, ins, scratch, keep, last_weights)
        combine(nc, ins, scratch, keep, last_weights, out)


def bf16_bits(a):
    bits = np.asarray(a, np.float32).view(np.uint32)
    return (bits >> 16).astype(np.uint16)


def constants():
    slopes = (2.0 ** (-8.0 * np.arange(1, NH + 1) / NH)).astype(np.float32)
    parts, rest = [], slopes.copy()
    for _ in range(3):
        top = (rest.view(np.uint32) & np.uint32(0xFFFF0000)).view(np.float32)
        parts.append(top)
        rest = rest - top
    c_q = np.zeros((NQ, 6, 4, S), np.float32)
    for j in range(6):
        c_q[:, j] = parts[j % 3].reshape(NQ, 4, 1)
    pos = np.arange(S)
    c_k = np.ones((9, 4, S), np.float32)
    c_k[0:3] = (pos // 256 * 256)[None, None, :]
    c_k[3:6] = (pos % 256)[None, None, :]
    return bf16_bits(c_q), bf16_bits(c_k)


def kernel(L0_attn_x, L0_attn_Wq, L0_attn_Wk, L0_attn_Wv, L0_attn_Wo, L0_attn_bo, L0_ffn_router_logits,
           L0_ffn_gating_einsum, L0_ffn_linear, L0_ffn_per_expert_scale, L0_ffn_router_scale):
    import concourse.bacc as bacc
    from concourse.bass_utils import run_bass_kernel_spmd

    split = lambda w: np.asarray(w).reshape(DH, P, -1).transpose(1, 0, 2)
    wq, wk = (split(w).reshape(P, DH, NQ, 4 * HD) for w in (L0_attn_Wq, L0_attn_Wk))
    w_gu = np.asarray(L0_ffn_gating_einsum).reshape(NE, 2 * HID, DH, P).transpose(3, 0, 2, 1)
    w_down = np.asarray(L0_ffn_linear).reshape(NE, DH, P, D).transpose(2, 0, 1, 3)
    c_q, c_k = constants()
    arrays = {
        "x": np.asarray(L0_attn_x).reshape(TOK, D),
        "w_qk": np.concatenate([wq, wk], axis=3),
        "w_v": split(L0_attn_Wv),
        "w_r": split(L0_ffn_router_logits),
        "router_scale": np.asarray(L0_ffn_router_scale).reshape(DH, P).T,
        "w_o": split(L0_attn_Wo),
        "bo": np.asarray(L0_attn_bo),
        "w_gu": w_gu.reshape(P, NE * DH, 2 * HID),
        "w_down": w_down.reshape(P, NE * DH, D),
        "expert_scale": np.asarray(L0_ffn_per_expert_scale),
        "c_q": c_q,
        "c_k": c_k,
    }
    arrays = {"in_" + k: np.ascontiguousarray(v) for k, v in arrays.items()}
    nc = bacc.Bacc("TRN2", target_bir_lowering=False, num_devices=1)
    ins = {}
    for name, a in arrays.items():
        ap = nc.dram_tensor(name, a.shape, mybir.dt.from_np(a.dtype), kind="ExternalInput").ap()
        ins[name[3:]] = ap.bitcast(BF16) if a.dtype == np.uint16 else ap
    out = nc.dram_tensor("out", (TOK, D), F32, kind="ExternalOutput").ap()
    build(nc, ins, out)
    r = run_bass_kernel_spmd(nc, [arrays], core_ids=[0])
    return r.results[0]["out"].reshape(B, S, D)
```
